# Optimizing a Trainium2 kernel written in Bass

```python
import numpy as np
import jax
import jax.numpy as jnp

def _softmax(x, axis=-1):
    return jax.nn.softmax(x, axis=axis)

def _gelu(x):
    return jax.nn.gelu(x, approximate=True)

def _silu(x):
    return jax.nn.silu(x)

def _sigmoid(x):
    return jax.nn.sigmoid(x)

def _layernorm(x, axis=-1, eps=1e-05):
    m = jnp.mean(x, axis=axis, keepdims=True)
    v = jnp.var(x, axis=axis, keepdims=True)
    return (x - m) / jnp.sqrt(v + eps)

def _scatter_add(tgt, idx, src, axis=0):
    return tgt.at[idx].add(src)

def _segment_sum(src, seg, n):
    return jax.ops.segment_sum(src, seg, n)
kernel_name = 'mk_gnn_resnorm_d2_gnn_r8_e573d4'

def setup_inputs(seed: int=0):
    np.random.seed(seed)
    _w = jnp.asarray

    def _rec_inputs():
        import jax
        import jax.numpy as jnp
        _gk = jax.random.key(seed)
        x = -1.686e-05 + 1 * jax.random.normal(jax.random.fold_in(_gk, 1), (6250, 160), jnp.float32)
        src = jax.random.randint(jax.random.fold_in(_gk, 2), (200000,), 0, 6250, jnp.int32)
        dst = jnp.minimum((6250 * jax.random.uniform(jax.random.fold_in(_gk, 3), (200000,)) ** 2.0).astype(jnp.int32), 49999)
        _o = jnp.argsort(dst, stable=True)
        src = src[_o]
        dst = dst[_o]
        edge_attr_12 = jax.random.uniform(jax.random.fold_in(_gk, 12), (200000, 12), jnp.float32, 0.0, 1)
        edge_attr_4 = 0.000486536 + 0.999406 * jax.random.normal(jax.random.fold_in(_gk, 13), (200000, 4), jnp.float32)
        edge_attr_8 = 0.000398945 + 1.00003 * jax.random.normal(jax.random.fold_in(_gk, 14), (200000, 8), jnp.float32)
        node_vec1 = jax.random.uniform(jax.random.fold_in(_gk, 15), (6250, 1), jnp.float32, 0.0, 0.999994)
        return (x, src, dst, edge_attr_12, edge_attr_4, edge_attr_8, node_vec1)
    x, src, dst, edge_attr_12, edge_attr_4, edge_attr_8, node_vec1 = _rec_inputs()

    def _L0_gnn_setup():
        import jax, jax.numpy as jnp
        import numpy as np
        N = 6250
        E = 50000
        MUL0 = 64
        MUL1 = 32
        NEF = 12
        RN = 100
        NUM_NEIGHBORS = 8.0
        WNUM = MUL0 + MUL0 + MUL1 + MUL1

        def _split(x):
            return (x[:, :MUL0], x[:, MUL0:].reshape(-1, MUL1, 3))

        def _fctp_scalar_attr(x0, x1, z, Ws, Wv):
            s = x0 @ Ws * z / np.sqrt(Ws.shape[0])
            v = jnp.einsum('nuc,uw->nwc', x1, Wv) * z[:, :, None] / np.sqrt(Wv.shape[0])
            return (s, v)
        key = jax.random.key(seed)
        ks = jax.random.split(key, 16)
        return {'node_input': jax.random.normal(ks[0], (N, MUL0 + 3 * MUL1), jnp.float32), 'node_attr': jax.random.uniform(ks[1], (N, 1), dtype=jnp.float32), 'edge_src': jax.random.randint(ks[2], (E,), 0, N), 'edge_dst': jax.random.randint(ks[3], (E,), 0, N), 'edge_attr': jax.random.normal(ks[4], (E, 4), jnp.float32), 'edge_features': jax.random.uniform(ks[5], (E, NEF), dtype=jnp.float32), 'W_sc0': jax.random.normal(ks[6], (MUL0, MUL0), jnp.float32), 'W_sc1': jax.random.normal(ks[7], (MUL1, MUL1), jnp.float32), 'W_l1_0': jax.random.normal(ks[8], (MUL0, MUL0), jnp.float32), 'W_l1_1': jax.random.normal(ks[9], (MUL1, MUL1), jnp.float32), 'W_fc1': jax.random.normal(ks[10], (NEF, RN), jnp.float32), 'W_fc2': jax.random.normal(ks[11], (RN, WNUM), jnp.float32), 'W_l2_0': jax.random.normal(ks[12], (MUL0 + MUL1, MUL0), jnp.float32), 'W_l2_1': jax.random.normal(ks[13], (MUL0 + MUL1, MUL1), jnp.float32)}
    _L0_gnn_all = _L0_gnn_setup()
    _L0_gnn_in = {k: v for k, v in _L0_gnn_all.items() if k in ('W_sc0', 'W_sc1', 'W_l1_0', 'W_l1_1', 'W_fc1', 'W_fc2', 'W_l2_0', 'W_l2_1')}
    del _L0_gnn_all

    def _L1_gnn_setup():
        import jax, jax.numpy as jnp
        import numpy as np
        INV3 = 1.0 / np.sqrt(3.0)

        def _fctp(x_s, x_v, attr, w0, w1):
            s = x_s @ w0 * (1.0 / np.sqrt(x_s.shape[-1])) * attr
            v = jnp.einsum('nud,uw->nwd', x_v, w1) * (1.0 / np.sqrt(x_v.shape[-2])) * attr[..., None]
            return (s, v)
        key = jax.random.key(seed)
        ks = jax.random.split(key, 16)
        N, E = (6250, 100000)
        inp = {'node_input': jax.random.normal(ks[0], (N, 160), jnp.float32), 'node_attr': jnp.ones((N, 1), jnp.float32), 'edge_attr': jax.random.normal(ks[1], (E, 4), jnp.float32), 'edge_scalars': jax.random.normal(ks[2], (E, 8), jnp.float32), 'sc_w0': jax.random.normal(ks[3], (64, 64), jnp.float32), 'sc_w1': jax.random.normal(ks[4], (32, 32), jnp.float32), 'lin1_w0': jax.random.normal(ks[5], (64, 64), jnp.float32), 'lin1_w1': jax.random.normal(ks[6], (32, 32), jnp.float32), 'fc_w1': jax.random.normal(ks[7], (8, 64), jnp.float32), 'fc_w2': jax.random.normal(ks[8], (64, 192), jnp.float32), 'lin2_w0': jax.random.normal(ks[9], (96, 64), jnp.float32), 'lin2_w1': jax.random.normal(ks[10], (96, 32), jnp.float32), 'lin3_w': jax.random.normal(ks[11], (96, 1), jnp.float32), 'edge_src': jax.random.randint(ks[12], (E,), 0, N), 'edge_dst': jax.random.randint(ks[13], (E,), 0, N), 'num_neighbors': 16}
        return inp
    _L1_gnn_all = _L1_gnn_setup()
    _L1_gnn_in = {k: v for k, v in _L1_gnn_all.items() if k in ('sc_w0', 'sc_w1', 'lin1_w0', 'lin1_w1', 'fc_w1', 'fc_w2', 'lin2_w0', 'lin2_w1', 'lin3_w')}
    del _L1_gnn_all
    return {'x': x, 'src': src, 'dst': dst, 'edge_attr_12': edge_attr_12, 'edge_attr_4': edge_attr_4, 'edge_attr_8': edge_attr_8, 'node_vec1': node_vec1, 'L0_gnn_W_sc0': _L0_gnn_in['W_sc0'], 'L0_gnn_W_sc1': _L0_gnn_in['W_sc1'], 'L0_gnn_W_l1_0': _L0_gnn_in['W_l1_0'], 'L0_gnn_W_l1_1': _L0_gnn_in['W_l1_1'], 'L0_gnn_W_fc1': _L0_gnn_in['W_fc1'], 'L0_gnn_W_fc2': _L0_gnn_in['W_fc2'], 'L0_gnn_W_l2_0': _L0_gnn_in['W_l2_0'], 'L0_gnn_W_l2_1': _L0_gnn_in['W_l2_1'], 'L1_gnn_sc_w0': _L1_gnn_in['sc_w0'], 'L1_gnn_sc_w1': _L1_gnn_in['sc_w1'], 'L1_gnn_lin1_w0': _L1_gnn_in['lin1_w0'], 'L1_gnn_lin1_w1': _L1_gnn_in['lin1_w1'], 'L1_gnn_fc_w1': _L1_gnn_in['fc_w1'], 'L1_gnn_fc_w2': _L1_gnn_in['fc_w2'], 'L1_gnn_lin2_w0': _L1_gnn_in['lin2_w0'], 'L1_gnn_lin2_w1': _L1_gnn_in['lin2_w1'], 'L1_gnn_lin3_w': _L1_gnn_in['lin3_w']}

def reference(x, src, dst, edge_attr_12, edge_attr_4, edge_attr_8, node_vec1, L0_gnn_W_sc0, L0_gnn_W_sc1, L0_gnn_W_l1_0, L0_gnn_W_l1_1, L0_gnn_W_fc1, L0_gnn_W_fc2, L0_gnn_W_l2_0, L0_gnn_W_l2_1, L1_gnn_sc_w0, L1_gnn_sc_w1, L1_gnn_lin1_w0, L1_gnn_lin1_w1, L1_gnn_fc_w1, L1_gnn_fc_w2, L1_gnn_lin2_w0, L1_gnn_lin2_w1, L1_gnn_lin3_w):
    import jax
    import jax.numpy as jnp

    def _L0_gnn_ref(node_input, node_attr, edge_src, edge_dst, edge_attr, edge_features, W_sc0, W_sc1, W_l1_0, W_l1_1, W_fc1, W_fc2, W_l2_0, W_l2_1):
        import jax, jax.numpy as jnp
        import numpy as np
        N = 6250
        E = 50000
        MUL0 = 64
        MUL1 = 32
        NEF = 12
        RN = 100
        NUM_NEIGHBORS = 8.0
        WNUM = MUL0 + MUL0 + MUL1 + MUL1

        def _split(x):
            return (x[:, :MUL0], x[:, MUL0:].reshape(-1, MUL1, 3))

        def _fctp_scalar_attr(x0, x1, z, Ws, Wv):
            s = x0 @ Ws * z / np.sqrt(Ws.shape[0])
            v = jnp.einsum('nuc,uw->nwc', x1, Wv) * z[:, :, None] / np.sqrt(Wv.shape[0])
            return (s, v)
        x0, x1 = _split(node_input)
        z = node_attr
        s0, s1 = _fctp_scalar_attr(x0, x1, z, W_sc0, W_sc1)
        h0, h1 = _fctp_scalar_attr(x0, x1, z, W_l1_0, W_l1_1)
        h = jax.nn.silu(edge_features @ W_fc1 / np.sqrt(NEF))
        w = h @ W_fc2 / np.sqrt(RN)
        w0 = w[:, :MUL0]
        w1 = w[:, MUL0:2 * MUL0]
        w2 = w[:, 2 * MUL0:2 * MUL0 + MUL1]
        w3 = w[:, 2 * MUL0 + MUL1:]
        e0 = h0[edge_src]
        e1 = h1[edge_src]
        y0 = edge_attr[:, :1]
        y1 = edge_attr[:, 1:]
        m0a = w0 * e0 * y0
        m0b = w3 * jnp.einsum('eui,ei->eu', e1, y1) / np.sqrt(3.0)
        m1a = (w1 * e0)[:, :, None] * y1[:, None, :]
        m1b = w2[:, :, None] * (e1 * y0[:, :, None])
        mid_s = jnp.concatenate([m0a, m0b], axis=1)
        mid_v = jnp.concatenate([m1a, m1b], axis=1)
        inv = 1.0 / np.sqrt(NUM_NEIGHBORS)
        ns = jax.ops.segment_sum(mid_s, edge_dst, num_segments=N) * inv
        nv = jax.ops.segment_sum(mid_v, edge_dst, num_segments=N) * inv
        o0, o1 = _fctp_scalar_attr(ns, nv, z, W_l2_0, W_l2_1)
        c_s, c_x = (np.sin(np.pi / 8), np.cos(np.pi / 8))
        out0 = c_s * s0 + c_x * o0
        out1 = c_s * s1 + c_x * o1
        return jnp.concatenate([out0, out1.reshape(N, -1)], axis=1)

    def _L1_gnn_ref(node_input, node_attr, edge_attr, edge_scalars, sc_w0, sc_w1, lin1_w0, lin1_w1, fc_w1, fc_w2, lin2_w0, lin2_w1, lin3_w, edge_src, edge_dst, num_neighbors):
        import jax, jax.numpy as jnp
        import numpy as np
        INV3 = 1.0 / np.sqrt(3.0)

        def _fctp(x_s, x_v, attr, w0, w1):
            s = x_s @ w0 * (1.0 / np.sqrt(x_s.shape[-1])) * attr
            v = jnp.einsum('nud,uw->nwd', x_v, w1) * (1.0 / np.sqrt(x_v.shape[-2])) * attr[..., None]
            return (s, v)
        N = node_input.shape[0]
        h = jax.nn.silu(edge_scalars @ fc_w1 * (1.0 / np.sqrt(8.0)))
        weight = h @ fc_w2 * (1.0 / np.sqrt(64.0))
        xs, xv = (node_input[:, :64], node_input[:, 64:].reshape(N, 32, 3))
        sc_s, sc_v = _fctp(xs, xv, node_attr, sc_w0, sc_w1)
        f_s, f_v = _fctp(xs, xv, node_attr, lin1_w0, lin1_w1)
        gs = f_s[edge_src]
        gv = f_v[edge_src]
        ys, yv = (edge_attr[:, :1], edge_attr[:, 1:])
        w1_, w2_ = (weight[:, :64], weight[:, 64:128])
        w3_, w4_ = (weight[:, 128:160], weight[:, 160:192])
        m0a = gs * ys * w1_
        m0b = jnp.sum(gv * yv[:, None, :], -1) * INV3 * w4_
        m1a = gs[..., None] * yv[:, None, :] * w2_[..., None]
        m1b = gv * ys[..., None] * w3_[..., None]
        E = m0a.shape[0]
        edge_feat = jnp.concatenate([m0a, m0b, m1a.reshape(E, 192), m1b.reshape(E, 96)], -1)
        mid = jax.ops.segment_sum(edge_feat, edge_dst, num_segments=N)
        mid = mid / np.sqrt(float(num_neighbors))
        mid_s, mid_v = (mid[:, :96], mid[:, 96:].reshape(N, 96, 3))
        c_s, c_v = _fctp(mid_s, mid_v, node_attr, lin2_w0, lin2_w1)
        conv = jnp.concatenate([c_s, c_v.reshape(N, -1)], -1)
        scfeat = jnp.concatenate([sc_s, sc_v.reshape(N, -1)], -1)
        angle = 0.1 * (mid_s @ lin3_w) * (1.0 / np.sqrt(96.0)) * node_attr
        return jnp.cos(angle) * scfeat + jnp.sin(angle) * conv
    x = _layernorm(x + _L0_gnn_ref(x, node_vec1, src, dst, edge_attr_4, edge_attr_12, L0_gnn_W_sc0, L0_gnn_W_sc1, L0_gnn_W_l1_0, L0_gnn_W_l1_1, L0_gnn_W_fc1, L0_gnn_W_fc2, L0_gnn_W_l2_0, L0_gnn_W_l2_1), axis=-1)
    x = _layernorm(x + _L1_gnn_ref(x, node_vec1, edge_attr_4, edge_attr_8, L1_gnn_sc_w0, L1_gnn_sc_w1, L1_gnn_lin1_w0, L1_gnn_lin1_w1, L1_gnn_fc_w1, L1_gnn_fc_w2, L1_gnn_lin2_w0, L1_gnn_lin2_w1, L1_gnn_lin3_w, src, dst, 16), axis=-1)
    return x

_drawn_inputs = setup_inputs


def setup_inputs(seed=0):
    import zlib

    import numpy as np

    out = dict(_drawn_inputs(seed))
    spreads = {}
    factors = {'edge_attr_8': 4.632,
     'L1_gnn_lin1_w0': 4.907,
     'L1_gnn_lin1_w1': 4.7,
     'L1_gnn_fc_w1': 4.134,
     'L1_gnn_fc_w2': 4.004,
     'L1_gnn_lin2_w0': 7.215,
     'L1_gnn_lin2_w1': 5.929,
     'L1_gnn_lin3_w': 4.555,
     'L1_gnn_sc_w0': 4.76,
     'L1_gnn_sc_w1': 3.853}
    for name, (base, spread) in spreads.items():
        noise = np.random.default_rng([zlib.crc32(name.encode()), seed]).standard_normal(out[name].shape)
        drawn = base * np.exp(spread * noise) if base else spread * noise
        out[name] = jnp.asarray(drawn.astype(out[name].dtype))
    for name, factor in factors.items():
        out[name] = (out[name] * factor).astype(out[name].dtype)
    return out
```

```python
from contextlib import ExitStack

import concourse.bass as bass
from concourse import mybir

F32 = mybir.dt.float32
I32 = mybir.dt.int32
ALU = mybir.AluOpType
ACT = mybir.ActivationFunctionType
AX_X = mybir.AxisListType.X

P = 128
N = 6250
E = 200000
S0, V0 = 64, 32
FEAT = S0 + 3 * V0
MID = 4 * (S0 + V0)
BLK = S0 + V0
WCOL = 2 * S0 + 2 * V0

QT = 4
GT = 8
NG = 2 * -(-E // (2 * GT * P))
T = NG * GT
NQ = T // QT
ITERS = NG // 2

CH = 5
NCH = 10
NT = CH * NCH
NPAD = NT * P
TRASH = NPAD - P
assert TRASH >= N and ITERS * 4 == NQ


def program(nc, t):
    layers = (
        dict(nef=12, hid=100, attr=t["attr12_t"], w1=t["L0_fc1"], w2=t["L0_fc2"], fc1_scale=12.0 ** -0.5,
             w2_scale=(100.0 * 8.0) ** -0.5, h_scale=1.0, sc_scale=float(0.3826834323650898),
             conv_scale=float(0.9238795325112867), lin1=(t["L0_l1_0"], t["L0_l1_1"]),
             sc=(t["L0_sc0"], t["L0_sc1"]), lin2=(t["L0_l2_0"], t["L0_l2_1"])),
        dict(nef=8, hid=64, attr=t["attr8_t"], w1=t["L1_fc1"], w2=t["L1_fc2"], fc1_scale=8.0 ** -0.5,
             w2_scale=(64.0 * 16.0) ** -0.5, h_scale=1.0, sc_scale=1.0, conv_scale=1.0,
             lin1=(t["L1_l1_0"], t["L1_l1_1"]), sc=(t["L1_sc0"], t["L1_sc1"]), lin2=(t["L1_l2_0"], t["L1_l2_1"])),
    )
    ctx = ExitStack()
    with ctx:
        def sb(name, shape, dt=F32):
            return ctx.enter_context(nc.sbuf_tensor(name, shape, dt))

        def sem(name):
            return ctx.enter_context(nc.semaphore(name))

        table = [nc.dram_tensor(f"table{l}", [NPAD, FEAT], F32, kind="Internal").ap() for l in range(2)]
        acc = [nc.dram_tensor(f"acc{l}", [NPAD, MID], F32, kind="Internal").ap() for l in range(2)]
        x1_t = nc.dram_tensor("x1_t", [FEAT, NPAD], F32, kind="Internal").ap()
        feat_t = (t["x_t"], x1_t)

        y_all = sb("y_all", [P, T, 4])
        dst_f = sb("dst_f", [P, T])
        dst_rel = sb("dst_rel", [P, T])
        base_f = sb("base_f", [P, NG])
        row_f = sb("row_f", [P, NG])
        x_all = sb("x_all", [P, NT, FEAT])
        z_all = sb("z_all", [P, NT])
        ident = sb("ident", [P, P])
        iota_r = sb("iota_r", [P, P])
        iota_p = sb("iota_p", [P, 1])
        below = sb("below", [P, P])
        zero_col = sb("zero_col", [P, 1])
        eps_col = sb("eps_col", [P, 1])
        w1s = [sb(f"w1s{l}", [layers[l]["nef"], layers[l]["hid"]]) for l in range(2)]
        w2s = [sb(f"w2s{l}", [layers[l]["hid"], WCOL]) for l in range(2)]
        lin1s = [(sb(f"lin1s{l}", [S0, S0]), sb(f"lin1v{l}", [3 * V0, 3 * V0])) for l in range(2)]
        scs = [(sb(f"scs{l}", [S0, S0]), sb(f"scv{l}", [3 * V0, 3 * V0])) for l in range(2)]
        lin2s = [(sb(f"lin2s{l}", [BLK, S0]), sb(f"lin2v{l}", [BLK, V0])) for l in range(2)]
        lin3 = sb("lin3", [BLK, 1])

        attr = sb("attr_sb", [12, 2, GT * P])
        src_i = sb("src_i", [P, 2, GT], I32)
        gath = sb("gath", [P, 2 * GT, FEAT])
        hid = sb("hid", [100, 2, QT * P])
        wy = sb("wy", [P, 2, QT, BLK])
        mul_p = sb("mul_p", [P, QT, S0])
        dot3 = sb("dot3", [P, QT, 3, V0])
        dot = sb("dot", [P, QT, V0])
        msg = sb("msg", [P, 2, QT, 4, BLK])
        onehot = sb("onehot", [P, 2, QT, P])
        flush = sb("flush", [P, 2, MID])
        flush_row = [sb(f"flush_row{b}", [P, 1], I32) for b in range(2)]
        mid = sb("mid", [P, 2, CH, MID])
        xt_s = sb("xt_s", [S0, 2, CH * P])
        xt_v = sb("xt_v", [3 * V0, 2, CH * P])
        mid_t = sb("mid_t", [BLK, 2, 4 * P])
        lin_o = sb("lin_o", [P, 2, CH, 2 * FEAT + 1])
        cen = sb("cen", [P, CH, FEAT])
        squ = sb("squ", [P, CH, FEAT])
        st = sb("st", [P, 16, CH])
        tab = sb("tab", [P, 2, CH, FEAT])
        dst_i = mid[:, :, :, :].rearrange("p b c m -> p (b c m)")[:, 0:T].bitcast(I32)
        base_i = lin_o[:, 0, :, :].rearrange("p c m -> p (c m)")[:, 0:NG].bitcast(I32)
        iota_ri = squ[:, 0, 0:P].bitcast(I32)
        iota_pi = squ[:, 1, 0:1].bitcast(I32)
        zeros = msg[:, :, :, :, :].rearrange("p a t b c -> p (a t b c)")
        lim = st[:, 0, 0:2]
        lim_t = sb("lim_t", [2, P])
        lim_r = sb("lim_r", [2, 4])
        flag_f = sb("flag_f", [1, 4])
        flag_i = sb("flag_i", [1, 1], I32)
        dst_row = sb("dst_row", [P, QT, P], I32)
        earlier = sb("earlier", [P, P])
        count = sb("count", [P, QT])
        row_g = sb("row_g", [P, QT])
        row_gi = [sb(f"row_gi{k}", [P, 1], I32) for k in range(QT)]
        src_g = sb("src_gen", [P, QT], I32)
        gflush = mid[:, 0, 0:QT, :]

        ps = ctx.enter_context(nc.psum_tensor("ps", [P, 8, 512], F32))

        in_loaded = sem("in_loaded")
        w_loaded = sem("w_loaded")
        zeroed = sem("zeroed")
        zeros_set = sem("zeros_set")
        iota_set = sem("iota_set")
        ident_set = sem("ident_set")
        setup_step = sem("setup_step")
        lim_turned = sem("lim_turned")
        lim_turned2 = sem("lim_turned2")
        flag_set = sem("flag_set")
        phase_end = sem("phase_end")
        phases = {}

        def phase_barrier(eng, name):
            phases[eng] = phases.get(eng, 0) + 1
            eng.drain().then_inc(phase_end, 1)
            eng.wait_ge(phase_end, 5 * phases[eng])

        def wait(eng, s, v):
            if isinstance(v, int) and v <= 0:
                return
            eng.wait_ge(s, v)

        passed = {}

        def settle(eng):
            if eng not in passed:
                passed[eng] = sem(f"passed{len(passed)}")
            eng.sem_inc(passed[eng], 1)

        class Sems:
            pass

        def table_sems(l):
            s = Sems()
            s.xt_in = [sem(f"l{l}_tab_xt_in{b}") for b in range(2)]
            s.mm = sem(f"l{l}_tab_mm")
            s.copied = sem(f"l{l}_tab_copied")
            s.stored = [sem(f"l{l}_tab_stored{b}") for b in range(2)]
            return s

        def edge_sems(l):
            s = Sems()
            s.attr_in = [sem(f"l{l}_attr_in{b}") for b in range(2)]
            s.src_in = [sem(f"l{l}_src_in{b}") for b in range(2)]
            s.gathered = [sem(f"l{l}_gathered{k}") for k in range(2 * GT)]
            s.fc1 = sem(f"l{l}_fc1")
            s.hid = sem(f"l{l}_hid")
            s.fc2 = sem(f"l{l}_fc2")
            s.wy = sem(f"l{l}_wy")
            s.chain = sem(f"l{l}_chain")
            s.msg = sem(f"l{l}_msg")
            s.seg = sem(f"l{l}_seg")
            s.evac = sem(f"l{l}_evac")
            s.added = [sem(f"l{l}_added{b}") for b in range(2)]
            return s

        def general_sems(l):
            s = Sems()
            s.start = sem(f"l{l}g_start")
            s.loaded = sem(f"l{l}g_loaded")
            s.gathered = [sem(f"l{l}g_gathered{k}") for k in range(QT)]
            s.fc1 = sem(f"l{l}g_fc1")
            s.hid = sem(f"l{l}g_hid")
            s.fc2 = sem(f"l{l}g_fc2")
            s.wy = sem(f"l{l}g_wy")
            s.chain = sem(f"l{l}g_chain")
            s.msg = sem(f"l{l}g_msg")
            s.seg = sem(f"l{l}g_seg")
            s.evac = sem(f"l{l}g_evac")
            s.added = sem(f"l{l}g_added")
            return s

        def node_sems(l):
            s = Sems()
            s.mid_in = [sem(f"l{l}_mid_in{b}") for b in range(2)]
            s.xt_in = [sem(f"l{l}_xt_in{b}") for b in range(2)]
            s.turned = sem(f"l{l}_turned")
            s.mid_t = sem(f"l{l}_mid_t")
            s.lin = sem(f"l{l}_lin")
            s.lin_o = sem(f"l{l}_lin_o")
            s.chain = sem(f"l{l}_node_chain")
            s.root = sem(f"l{l}_root")
            s.ang = sem(f"l{l}_ang")
            s.trig = sem(f"l{l}_trig")
            s.var = sem(f"l{l}_var")
            s.x = sem(f"l{l}_x")
            s.xturn = sem(f"l{l}_xturn")
            s.xt = sem(f"l{l}_xt")
            s.tab_mm = sem(f"l{l}_nt_mm")
            s.tab = sem(f"l{l}_nt_tab")
            s.stored = [sem(f"l{l}_stored{b}") for b in range(2)]
            s.xt_stored = [sem(f"l{l}_xt_stored{b}") for b in range(2)]
            return s

        tabs = table_sems(0)
        edges = [edge_sems(l) for l in range(2)]
        gens = [general_sems(l) for l in range(2)]
        nodes = [node_sems(l) for l in range(2)]

        ps_hid = [ps[:, b, :] for b in range(2)]
        ps_w = [ps[:, 2 + 2 * b:4 + 2 * b, :].rearrange("p a c -> p (a c)").rearrange("p (t c) -> p t c", t=QT)
                for b in range(2)]
        ps_acc = [ps[:, 6 + b, 0:MID] for b in range(2)]

        def loop(eng, body, iters):
            body(0)
            with eng.Fori(1, iters - 1) as it:
                body(it)
            body(iters - 1)

        def sp_setup(sp):
            sp.dma_start(dst_i, t["dst_pt"]).then_inc(in_loaded, 16)
            sp.dma_start(base_i, t["dst_first"].partition_broadcast(P)).then_inc(in_loaded, 16)
            sp.dma_start(z_all[:, :], t["z"]).then_inc(in_loaded, 16)
            sp.dma_start(x_all[:, :, :], t["x_rows"]).then_inc(in_loaded, 16)
            sp.dma_start(y_all[:, :, :], t["y"]).then_inc(in_loaded, 16)

        IN_DMAS = 5

        def act_setup(act):
            n = 0
            for l, L in enumerate(layers):
                for dst, src in ((w1s[l], L["w1"]), (w2s[l], L["w2"]), (lin1s[l][0], L["lin1"][0]),
                                 (lin1s[l][1], L["lin1"][1]), (scs[l][0], L["sc"][0]), (scs[l][1], L["sc"][1]),
                                 (lin2s[l][0], L["lin2"][0]), (lin2s[l][1], L["lin2"][1])):
                    act.dma_start(dst[:, :], src).then_inc(w_loaded, 16)
                    n += 1
            act.dma_start(lin3[:, :], t["L1_lin3"]).then_inc(w_loaded, 16)
            n += 1
            act.wait_ge(zeros_set, 1)
            for l in range(2):
                per = zeros.shape[1] // MID
                rows = acc[l].rearrange("(p r) m -> p r m", p=P)
                done = 0
                while done < NT:
                    k = min(per, NT - done)
                    act.dma_start(rows[:, done:done + k, :],
                                  zeros[:, 0:k * MID].rearrange("p (r m) -> p r m", m=MID)).then_inc(zeroed, 16)
                    done += k

        ZERO_DMAS = 2 * -(-NT // (2 * QT))
        W_DMAS = 17

        def dve_setup(dve):
            c = [0]

            def link(ins):
                c[0] += 1
                ins.then_inc(setup_step, 1)
                dve.wait_ge(setup_step, c[0])

            nc.vector.memset(zeros, 0.0).then_inc(zeros_set, 1)
            nc.vector.memset(zero_col[:, :], 0.0)
            nc.vector.memset(eps_col[:, :], 1e-5)
            dve.wait_ge(iota_set, 2)
            nc.vector.tensor_copy(iota_r[:, :], iota_ri)
            link(nc.vector.tensor_copy(iota_p[:, :], iota_pi))
            nc.vector.tensor_scalar(ident[:, :], iota_r[:, :], iota_p[:, 0:1], None, ALU.is_equal).then_inc(ident_set, 1)
            nc.vector.tensor_scalar(below[:, :], iota_r[:, :], iota_p[:, 0:1], None, ALU.is_lt)
            dve.wait_ge(in_loaded, 16 * IN_DMAS)
            nc.vector.tensor_copy(dst_f[:, :], dst_i)
            link(nc.vector.tensor_copy(base_f[:, :], base_i))
            link(nc.vector.tensor_tensor(dst_rel[:, :].rearrange("p (g k) -> p g k", k=GT),
                                         dst_f[:, :].rearrange("p (g k) -> p g k", k=GT),
                                         base_f[:, :].unsqueeze(2).to_broadcast([P, NG, GT]), ALU.subtract))
            link(nc.vector.tensor_scalar(row_f[:, :], base_f[:, :], iota_p[:, 0:1], None, ALU.add))
            nc.vector.tensor_reduce(lim[:, 0:1], dst_rel[:, :], AX_X, ALU.max)
            link(nc.vector.tensor_reduce(lim[:, 1:2], dst_rel[:, :], AX_X, ALU.min))
            link(nc.vector.tensor_scalar(lim[:, 1:2], lim[:, 1:2], -1.0, float(P - 1), ALU.mult, ALU.add))
            dve.wait_ge(lim_turned, 1)
            link(nc.vector.tensor_reduce(lim_r[:, 0:1], ps[0:2, 0, 0:P], AX_X, ALU.max))
            dve.wait_ge(lim_turned2, 1)
            link(nc.vector.tensor_reduce(flag_f[:, 0:1], ps[0:1, 1, 0:2], AX_X, ALU.max))
            link(nc.vector.tensor_reduce(flag_f[:, 1:2], base_f[0:1, :], AX_X, ALU.max))
            link(nc.vector.tensor_scalar(flag_f[:, 1:2], flag_f[:, 1:2], float(N), None, ALU.is_ge))
            link(nc.vector.tensor_scalar(flag_f[:, 0:1], flag_f[:, 0:1], float(P), None, ALU.is_ge))
            link(nc.vector.tensor_tensor(flag_f[:, 2:3], flag_f[:, 0:1], flag_f[:, 1:2], ALU.max))
            nc.vector.tensor_copy(flag_i[:, :], flag_f[:, 2:3]).then_inc(flag_set, 1)
            dve.wait_ge(w_loaded, 16 * W_DMAS)
            for l, L in enumerate(layers):
                nc.vector.tensor_scalar(w2s[l][:, :], w2s[l][:, :], L["w2_scale"], None, ALU.mult).then_inc(setup_step, 1)
                for (ws, wv), k in ((lin1s[l], 1.0), (scs[l], L["sc_scale"])):
                    nc.vector.tensor_scalar(ws[:, :], ws[:, :], k * S0 ** -0.5, None, ALU.mult).then_inc(setup_step, 1)
                    nc.vector.tensor_scalar(wv[:, :], wv[:, :], k * V0 ** -0.5, None, ALU.mult).then_inc(setup_step, 1)
                for w in lin2s[l]:
                    nc.vector.tensor_scalar(w[:, :], w[:, :], L["conv_scale"] * BLK ** -0.5, None,
                                            ALU.mult).then_inc(setup_step, 1)
                c[0] += 7
                dve.wait_ge(setup_step, c[0])
                link(nc.vector.tensor_scalar(w2s[l][:, WCOL - V0:WCOL], w2s[l][:, WCOL - V0:WCOL], 3.0 ** -0.5, None,
                                             ALU.mult))
            link(nc.vector.tensor_scalar(lin3[:, :], lin3[:, :], 0.1 * BLK ** -0.5, None, ALU.mult))

        def pool_setup(pool):
            nc.gpsimd.iota(iota_ri, pattern=[[1, P]], base=0, channel_multiplier=0).then_inc(iota_set, 1)
            nc.gpsimd.iota(iota_pi, pattern=[[0, 1]], base=0, channel_multiplier=1).then_inc(iota_set, 1)

        def pe_setup(pe):
            pe.wait_ge(ident_set, 1)
            pe.wait_ge(setup_step, 6)
            nc.tensor.transpose(ps[0:2, 0, 0:P], lim, ident[:, :]).then_inc(lim_turned, 1)
            pe.wait_ge(setup_step, 7)
            nc.tensor.transpose(ps[0:1, 1, 0:2], lim_r[:, 0:1], ident[0:2, 0:2]).then_inc(lim_turned2, 1)

        def tab_loads(sp):
            def body(it):
                for b in range(2):
                    wait(sp, tabs.mm, (2 * it + b - 1) * CH)
                    settle(sp)
                    cols = bass.ds((2 * it + b) * CH * P, CH * P)
                    sp.dma_start(xt_s[:, b, :], feat_t[0][0:S0, cols]).then_inc(tabs.xt_in[b], 16)
                    sp.dma_start(xt_v[:, b, :], feat_t[0][S0:FEAT, cols]).then_inc(tabs.xt_in[b], 16)
            loop(sp, body, NCH // 2)

        def table_mm(out, l, b, i):
            c = slice(i * P, (i + 1) * P)
            nc.tensor.matmul(out[:, 0:S0], xt_s[:, b, c], lin1s[l][0][:, :], start=True, stop=True)
            return nc.tensor.matmul(out[:, S0:FEAT], xt_v[:, b, c], lin1s[l][1][:, :], start=True, stop=True)

        def tab_pe(pe):
            def body(it):
                for b in range(2):
                    pe.wait_ge(tabs.xt_in[b], 32 * (it + 1))
                    for i in range(CH):
                        n = (2 * it + b) * CH + i
                        k = b * CH + i
                        wait(pe, tabs.copied, n - 1)
                        table_mm(ps[:, 6 + k % 2, :], 0, b, i).then_inc(tabs.mm, 1)
            loop(pe, body, NCH // 2)

        def tab_act(act):
            def body(it):
                for b in range(2):
                    wait(act, tabs.stored[b], 16 * it)
                    for i in range(CH):
                        n = (2 * it + b) * CH + i
                        k = b * CH + i
                        act.wait_ge(tabs.mm, n + 1)
                        nc.scalar.activation(tab[:, b, i, :], ps[:, 6 + k % 2, 0:FEAT], ACT.Copy,
                                             scale=z_all[:, bass.ds(n, 1)]).then_inc(tabs.copied, 1)
            loop(act, body, NCH // 2)

        def store_table(eng, l, b, ch, done):
            eng.dma_start(table[l].rearrange("(n p) f -> p n f", p=P)[:, bass.ds(ch * CH, CH), :],
                          tab[:, b, :, :]).then_inc(done, 16)

        def tab_pool(pool):
            def body(it):
                for b in range(2):
                    pool.wait_ge(tabs.copied, (2 * it + b + 1) * CH)
                    settle(pool)
                    store_table(pool, 0, b, 2 * it + b, tabs.stored[b])
            loop(pool, body, NCH // 2)
            for b in range(2):
                pool.wait_ge(tabs.stored[b], 16 * (NCH // 2))

        def edge_sp(sp, l):
            s, L = edges[l], layers[l]

            def body(it):
                for b in range(2):
                    g = 2 * it + b
                    wait(sp, s.fc1, 4 * it + 2 * b - 2)
                    settle(sp)
                    sp.dma_start(attr[0:L["nef"], b, :], L["attr"][:, bass.ds(g * GT * P, GT * P)]).then_inc(
                        s.attr_in[b], 16)
                    for k in range(GT):
                        wait(sp, s.gathered[GT * b + k], 16 * it)
                    settle(sp)
                    sp.dma_start(src_i[:, b, :], t["src_g"][bass.ds(g, 1), :, :].rearrange("g p k -> p (g k)")
                                 ).then_inc(s.src_in[b], 16)
            loop(sp, body, ITERS)

        def edge_pool(pool, l):
            s = edges[l]

            def add_group(g, b, it):
                pool.wait_ge(s.evac, g + 1)
                if not (isinstance(g, int) and g == 0):
                    pool.wait_ge(s.added[1 - b], 16 * (it if b == 0 else it + 1))
                settle(pool)
                pool.indirect_dma_start(acc[l], bass.IndirectOffsetOnAxis(ap=flush_row[b][:, :], axis=0),
                                        flush[:, b, :], None, compute_op=ALU.add).then_inc(s.added[b], 16)

            def body(it):
                for b in range(2):
                    pool.wait_ge(s.src_in[b], 16 * (it + 1))
                    for k in range(GT):
                        if k % QT == 0:
                            wait(pool, s.msg, 4 * it + 2 * b + k // QT - 3)
                            settle(pool)
                        pool.indirect_dma_start(gath[:, GT * b + k, :], None, table[l],
                                                bass.IndirectOffsetOnAxis(ap=src_i[:, b, k:k + 1], axis=0)
                                                ).then_inc(s.gathered[GT * b + k], 16)
                    if not isinstance(it, int) or it > 0:
                        add_group(2 * it + b - 2, b, it - 1)
            loop(pool, body, ITERS)
            for b in range(2):
                add_group(NG - 2 + b, b, ITERS - 1)
            for b in range(2):
                pool.wait_ge(s.added[b], 16 * ITERS)

        def fc1_mm(L, l, b, rhs):
            return nc.tensor.matmul(ps_hid[b][0:L["hid"], :], w1s[l][:, :], rhs, start=True, stop=True)

        def fc2_mm(L, l, b):
            for k in range(QT):
                ins = nc.tensor.matmul(ps_w[b][:, k, 0:WCOL], hid[0:L["hid"], b, k * P:(k + 1) * P], w2s[l][:, :],
                                       start=True, stop=True)
            return ins

        def edge_pe(pe, l):
            s, L = edges[l], layers[l]

            def fc1(k, j, it):
                b = (j // 2) % 2
                if j % 2 == 0:
                    pe.wait_ge(s.attr_in[b], 16 * (it + j // 4 + 1))
                wait(pe, s.hid, k - 1)
                fc1_mm(L, l, j % 2, attr[0:L["nef"], b, (j % 2) * QT * P:(j % 2 + 1) * QT * P]).then_inc(s.fc1, 1)

            def fc2(k, j):
                pe.wait_ge(s.hid, k + 1)
                wait(pe, s.msg, k - 1)
                fc2_mm(L, l, j % 2).then_inc(s.fc2, 1)

            fc1(0, 0, 0)
            fc1(1, 1, 0)
            fc2(0, 0)

            def body(it):
                for j in range(4):
                    k = 4 * it + j
                    if not (isinstance(it, int) and k + 2 >= NQ):
                        fc1(k + 2, j + 2, it)
                    if not (isinstance(it, int) and k + 1 >= NQ):
                        fc2(k + 1, j + 1)
                    g = 2 * it + j // 2
                    if j % 2 == 0:
                        wait(pe, s.evac, g - 1)
                    pe.wait_ge(s.msg, k + 1)
                    for q in range(QT):
                        ins = nc.tensor.matmul(ps_acc[j // 2], onehot[:, j % 2, q, :],
                                               msg[:, j % 2, q, :, :].rearrange("p a c -> p (a c)"),
                                               start=(j % 2 == 0 and q == 0), stop=(j % 2 == 1 and q == QT - 1))
                    ins.then_inc(s.seg, 1)
            loop(pe, body, ITERS)

        def silu(L, b):
            return nc.scalar.activation(hid[0:L["hid"], b, :], ps_hid[b][0:L["hid"], :], ACT.Silu,
                                        scale=L["fc1_scale"])

        def wy_copy(b, tile0):
            for k in range(QT):
                ins = nc.scalar.activation(wy[:, b, k, :], ps_w[b][:, k, 0:BLK], ACT.Copy,
                                           scale=y_all[:, bass.ds(tile0 + k, 1), 0:1].rearrange("p a b -> p (a b)"))
            return ins

        def edge_act(act, l):
            s, L = edges[l], layers[l]

            def hidden(k, j):
                act.wait_ge(s.fc1, k + 1)
                wait(act, s.fc2, k - 1)
                silu(L, j % 2).then_inc(s.hid, 1)

            def weights(k, j):
                act.wait_ge(s.fc2, k + 1)
                wait(act, s.msg, k - 1)
                wy_copy(j % 2, k * QT).then_inc(s.wy, 1)

            hidden(0, 0)
            hidden(1, 1)
            weights(0, 0)

            def body(it):
                for j in range(4):
                    k = 4 * it + j
                    if not (isinstance(it, int) and k + 2 >= NQ):
                        hidden(k + 2, j)
                    if not (isinstance(it, int) and k + 1 >= NQ):
                        weights(k + 1, j + 1)
                    if j % 2 == 1:
                        b = j // 2
                        g = 2 * it + b
                        wait(act, s.added[b], 16 * it)
                        nc.scalar.activation(flush_row[b][:, :], row_f[:, bass.ds(g, 1)], ACT.Copy)
                        act.wait_ge(s.seg, k + 1)
                        nc.scalar.activation(flush[:, b, :], ps_acc[b], ACT.Copy).then_inc(s.evac, 1)
            loop(act, body, ITERS)

        def messages(dve, chain, wait_chain, b, g, tile0):
            h0 = g[:, :, 0:S0]
            h1 = g[:, :, S0:FEAT].rearrange("p t (i u) -> p t i u", i=3)
            yv = y_all[:, bass.ds(tile0, QT), 1:4]
            w = ps_w[b]
            m = msg[:, b, :, :, :]
            mult = ALU.mult
            nc.vector.tensor_tensor(dot3[:, :, :, :], h1, yv.unsqueeze(3).to_broadcast([P, QT, 3, V0]),
                                    mult).then_inc(chain, 1)
            nc.vector.tensor_tensor(mul_p[:, :, :], w[:, :, BLK:BLK + S0], h0, mult).then_inc(chain, 1)
            wait_chain(1)
            nc.vector.tensor_tensor(dot[:, :, :], dot3[:, :, 0, :], dot3[:, :, 1, :], ALU.add).then_inc(chain, 1)
            wait_chain(2)
            nc.vector.tensor_tensor(m[:, :, 1:4, 0:S0], mul_p[:, :, :].unsqueeze(2).to_broadcast([P, QT, 3, S0]),
                                    yv.unsqueeze(3).to_broadcast([P, QT, 3, S0]), mult)
            wait_chain(3)
            nc.vector.tensor_tensor(dot[:, :, :], dot[:, :, :], dot3[:, :, 2, :], ALU.add).then_inc(chain, 1)
            nc.vector.tensor_tensor(m[:, :, 0, 0:S0], wy[:, b, :, 0:S0], h0, mult)
            nc.vector.tensor_tensor(m[:, :, 1:4, S0:BLK], wy[:, b, :, S0:BLK].unsqueeze(2).to_broadcast([P, QT, 3, V0]),
                                    h1, mult)
            wait_chain(4)
            return nc.vector.tensor_tensor(m[:, :, 0, S0:BLK], w[:, :, BLK + S0:WCOL], dot[:, :, :], mult)

        def edge_dve(dve, l):
            s = edges[l]

            def body(it):
                for j in range(4):
                    k = 4 * it + j
                    wait(dve, s.seg, k - 1)
                    nc.vector.tensor_tensor(
                        onehot[:, j % 2, :, :], iota_r[:, :].unsqueeze(1).to_broadcast([P, QT, P]),
                        dst_rel[:, bass.ds(k * QT, QT)].unsqueeze(2).to_broadcast([P, QT, P]), ALU.is_equal)
                    for q in range(QT):
                        dve.wait_ge(s.gathered[QT * j + q], 16 * (it + 1))
                    dve.wait_ge(s.wy, k + 1)
                    messages(dve, s.chain, lambda n: dve.wait_ge(s.chain, k * 4 + n), j % 2,
                             gath[:, QT * j:QT * (j + 1), :], k * QT).then_inc(s.msg, 1)
            loop(dve, body, ITERS)

        def general_sp(sp, l):
            s, L = gens[l], layers[l]
            with sp.Fori(0, NQ) as k:
                sp.wait_ge(s.start, k + 1)
                settle(sp)
                sp.dma_start(attr[0:L["nef"], 0, 0:QT * P], L["attr"][:, bass.ds(k * QT * P, QT * P)]).then_inc(s.loaded, 16)
                sp.dma_start(src_g[:, :], t["src_q"][bass.ds(k, 1), :, :].rearrange("g p k -> p (g k)")).then_inc(s.loaded, 16)
                sp.dma_start(dst_row[:, :, :].rearrange("p t e -> p (t e)"),
                             t["dst_flat"][:, bass.ds(k * QT * P, QT * P)].rearrange("a e -> (a e)").partition_broadcast(P)
                             ).then_inc(s.loaded, 16)

        def general_pool(pool, l):
            s = gens[l]
            pool.sem_inc(s.start, 1)
            with pool.Fori(0, NQ) as k:
                pool.wait_ge(s.loaded, 48 * (k + 1))
                settle(pool)
                for q in range(QT):
                    pool.indirect_dma_start(gath[:, q, :], None, table[l],
                                            bass.IndirectOffsetOnAxis(ap=src_g[:, q:q + 1], axis=0)
                                            ).then_inc(s.gathered[q], 16)
                pool.wait_ge(s.evac, k + 1)
                settle(pool)
                for q in range(QT):
                    pool.indirect_dma_start(acc[l], bass.IndirectOffsetOnAxis(ap=row_gi[q][:, :], axis=0),
                                            gflush[:, q, :], None, compute_op=ALU.add).then_inc(s.added, 16)
                    pool.wait_ge(s.added, 16 * (k * QT + q + 1))
                    settle(pool)
                pool.sem_inc(s.start, 1)

        def general_pe(pe, l):
            s, L = gens[l], layers[l]
            with pe.Fori(0, NQ) as k:
                pe.wait_ge(s.loaded, 48 * (k + 1))
                fc1_mm(L, l, 0, attr[0:L["nef"], 0, 0:QT * P]).then_inc(s.fc1, 1)
                pe.wait_ge(s.hid, k + 1)
                fc2_mm(L, l, 0).then_inc(s.fc2, 1)
                pe.wait_ge(s.msg, k + 1)
                for q in range(QT):
                    ins = nc.tensor.matmul(ps[:, 4 + q, 0:MID], onehot[:, 0, q, :],
                                           msg[:, 0, q, :, :].rearrange("p a c -> p (a c)"), start=True, stop=True)
                ins.then_inc(s.seg, 1)

        def general_act(act, l):
            s, L = gens[l], layers[l]
            with act.Fori(0, NQ) as k:
                act.wait_ge(s.fc1, k + 1)
                silu(L, 0).then_inc(s.hid, 1)
                act.wait_ge(s.fc2, k + 1)
                wy_copy(0, k * QT).then_inc(s.wy, 1)
                act.wait_ge(s.seg, k + 1)
                for q in range(QT):
                    nc.scalar.activation(row_gi[q][:, :], row_g[:, q:q + 1], ACT.Copy)
                nc.scalar.activation(gflush, ps[:, 4:4 + QT, 0:MID], ACT.Copy).then_inc(s.evac, 1)

        def general_dve(dve, l):
            s = gens[l]
            with dve.Fori(0, NQ) as k:
                c = [4]

                def link(ins):
                    c[0] += 1
                    ins.then_inc(s.chain, 1)
                    dve.wait_ge(s.chain, k * LINKS + c[0])

                LINKS = 4 + QT + QT + 4
                dve.wait_ge(s.loaded, 48 * (k + 1))
                for q in range(QT):
                    dve.wait_ge(s.gathered[q], 16 * (k + 1))
                dve.wait_ge(s.wy, k + 1)
                messages(dve, s.chain, lambda n: dve.wait_ge(s.chain, k * LINKS + n), 0, gath[:, 0:QT, :], k * QT)
                dst_q = dst_f[:, bass.ds(k * QT, QT)]
                for q in range(QT):
                    link(nc.vector.tensor_tensor(onehot[:, 0, q, :], dst_row[:, q, :],
                                                 dst_f[:, bass.ds(k * QT + q, 1)].to_broadcast([P, P]), ALU.is_equal))
                    nc.vector.tensor_tensor(earlier[:, :], onehot[:, 0, q, :], below[:, :], ALU.mult).then_inc(s.chain, 1)
                    c[0] += 1
                    dve.wait_ge(s.chain, k * LINKS + c[0])
                    nc.vector.tensor_reduce(count[:, q:q + 1], earlier[:, :], AX_X, ALU.max)
                link(nc.vector.tensor_scalar(row_g[:, :], dst_q, float(N), None, ALU.is_ge))
                link(nc.vector.tensor_tensor(count[:, :], count[:, :], row_g[:, :], ALU.max))
                link(nc.vector.tensor_tensor(row_g[:, :], iota_p[:, 0:1].to_broadcast([P, QT]), dst_q, ALU.subtract))
                nc.vector.tensor_scalar(row_g[:, :], row_g[:, :], float(TRASH), None, ALU.add).then_inc(s.chain, 1)
                c[0] += 1
                dve.wait_ge(s.chain, k * LINKS + c[0])
                nc.vector.tensor_tensor(row_g[:, :], row_g[:, :], count[:, :], ALU.mult).then_inc(s.msg, 0) if False else None
                assert c[0] == LINKS
                nc.vector.tensor_tensor(row_g[:, :], row_g[:, :], count[:, :], ALU.mult).then_inc(s.fin, 1)
                dve.wait_ge(s.fin, k + 1)
                nc.vector.tensor_tensor(row_g[:, :], row_g[:, :], dst_q, ALU.add).then_inc(s.msg, 1)

        for l in range(2):
            gens[l].fin = sem(f"l{l}g_fin")

        def node_sp(sp, l):
            s = nodes[l]

            def body(it):
                for b in range(2):
                    ch = 2 * it + b
                    wait(sp, s.turned, (ch - 1) * CH)
                    settle(sp)
                    sp.dma_start(mid[:, b, :, :], acc[l].rearrange("(n p) m -> p n m", p=P)[:, bass.ds(ch * CH, CH), :]
                                 ).then_inc(s.mid_in[b], 16)
                    wait(sp, s.lin, (ch - 1) * CH)
                    settle(sp)
                    if l == 0 and not (isinstance(it, int) and it == 0):
                        sp.wait_ge(s.xt_stored[b], 32 * it)
                        settle(sp)
                        sp.wait_ge(s.tab_mm, (ch - 1) * CH)
                    cols = bass.ds(ch * CH * P, CH * P)
                    settle(sp)
                    sp.dma_start(xt_s[:, b, :], feat_t[l][0:S0, cols]).then_inc(s.xt_in[b], 16)
                    sp.dma_start(xt_v[:, b, :], feat_t[l][S0:FEAT, cols]).then_inc(s.xt_in[b], 16)
            loop(sp, body, NCH // 2)

        def node_pe(pe, l):
            s = nodes[l]

            def front(it, b):
                ch = 2 * it + b
                pe.wait_ge(s.mid_in[b], 16 * (it + 1))
                pe.wait_ge(s.xt_in[b], 32 * (it + 1))

                def turn(i):
                    n, k = ch * CH + i, (b * CH + i) % 2
                    wait(pe, s.mid_t, n - 1)
                    for q in range(4):
                        ins = nc.tensor.transpose(ps[0:BLK, k, q * P:(q + 1) * P], mid[:, b, i, q * BLK:(q + 1) * BLK],
                                                  ident[:, :])
                    ins.then_inc(s.turned, 1)

                def lin(i):
                    n, k = ch * CH + i, (b * CH + i) % 2
                    c = slice(i * P, (i + 1) * P)
                    o = ps[:, 2 + k, :]
                    wait(pe, s.lin_o, n - 1)
                    nc.tensor.matmul(o[:, 0:S0], xt_s[:, b, c], scs[l][0][:, :], start=True, stop=True)
                    nc.tensor.matmul(o[:, S0:FEAT], xt_v[:, b, c], scs[l][1][:, :], start=True, stop=True)
                    pe.wait_ge(s.mid_t, n + 1)
                    ms = mid_t[:, k, 0:P]
                    ins = nc.tensor.matmul(o[:, FEAT:FEAT + S0], ms, lin2s[l][0][:, :], start=True, stop=True)
                    if l == 1:
                        ins = nc.tensor.matmul(o[:, 2 * FEAT:2 * FEAT + 1], ms, lin3[:, :], start=True, stop=True)
                    for q in range(3):
                        c0 = FEAT + S0 + q * V0
                        ins = nc.tensor.matmul(o[:, c0:c0 + V0], mid_t[:, k, (q + 1) * P:(q + 2) * P],
                                               lin2s[l][1][:, :], start=True, stop=True)
                    ins.then_inc(s.lin, 1)

                turn(0)
                for i in range(CH):
                    if i + 1 < CH:
                        turn(i + 1)
                    lin(i)

            def tail(it, b):
                ch = 2 * it + b
                pe.wait_ge(s.x, ch + 1)
                for i in range(CH):
                    n, k = ch * CH + i, (b * CH + i) % 2
                    wait(pe, s.xt, n - 1)
                    settle(pe)
                    nc.tensor.transpose(ps[0:S0, 4 + k, 0:P], tab[:, b, i, 0:S0], ident[:, :])
                    nc.tensor.transpose(ps[0:3 * V0, 4 + k, P:2 * P], tab[:, b, i, S0:FEAT], ident[:, :]
                                        ).then_inc(s.xturn, 1)
                for i in range(CH):
                    n, k = ch * CH + i, (b * CH + i) % 2
                    pe.wait_ge(s.xt, n + 1)
                    wait(pe, s.tab, n - 1)
                    table_mm(ps[:, 6 + k, :], 1, b, i).then_inc(s.tab_mm, 1)

            def body(it):
                for b in range(2):
                    front(it, b)
                    if l == 0:
                        tail(it, b)
            loop(pe, body, NCH // 2)

        def node_act(act, l):
            s = nodes[l]

            def body(it):
                for b in range(2):
                    ch = 2 * it + b
                    for i in range(CH):
                        n, k = ch * CH + i, (b * CH + i) % 2
                        act.wait_ge(s.turned, n + 1)
                        wait(act, s.lin, n - 1)
                        nc.scalar.activation(mid_t[:, k, :], ps[0:BLK, k, :], ACT.Copy).then_inc(s.mid_t, 1)
                        act.wait_ge(s.lin, n + 1)
                        if i == 0:
                            wait(act, s.x, ch - 1)
                        cols = 2 * FEAT + l
                        nc.scalar.activation(lin_o[:, b, i, 0:cols], ps[:, 2 + k, 0:cols], ACT.Copy).then_inc(s.lin_o, 1)
                    if l == 1:
                        act.wait_ge(s.ang, ch + 1)
                        nc.scalar.activation(st[:, 8:10, :], st[:, 6:8, :], ACT.Sin, bias=zero_col[:, 0:1]).then_inc(s.trig, 1)
                    act.wait_ge(s.var, ch + 1)
                    nc.scalar.activation(st[:, 2, :], st[:, 1, :], ACT.Sqrt, bias=eps_col[:, 0:1], scale=1.0 / FEAT
                                         ).then_inc(s.root, 1)
                    if l == 0:
                        for i in range(CH):
                            n, k = ch * CH + i, (b * CH + i) % 2
                            act.wait_ge(s.xturn, n + 1)
                            c = slice(i * P, (i + 1) * P)
                            nc.scalar.activation(xt_s[:, b, c], ps[0:S0, 4 + k, 0:P], ACT.Copy)
                            nc.scalar.activation(xt_v[:, b, c], ps[0:3 * V0, 4 + k, P:2 * P], ACT.Copy).then_inc(s.xt, 1)
                        for i in range(CH):
                            n, k = ch * CH + i, (b * CH + i) % 2
                            act.wait_ge(s.tab_mm, n + 1)
                            nc.scalar.activation(tab[:, b, i, :], ps[:, 6 + k, 0:FEAT], ACT.Copy,
                                                 scale=z_all[:, bass.ds(n, 1)]).then_inc(s.tab, 1)
            loop(act, body, NCH // 2)

        TWO_PI = 6.283185307179586
        PI_A = 6.28125
        PI_B = 0.0019350051879882812
        PI_C = TWO_PI - PI_A - PI_B
        ROUND = 12582912.0

        def node_dve(dve, l):
            s = nodes[l]
            v = nc.vector
            LINKS = 9 if l == 0 else 19

            def body(it):
                for b in range(2):
                    ch = 2 * it + b
                    c = [0]

                    def link(ins):
                        c[0] += 1
                        ins.then_inc(s.chain, 1)
                        dve.wait_ge(s.chain, ch * LINKS + c[0])

                    def per_node(a):
                        return a.unsqueeze(2).to_broadcast([P, CH, FEAT])

                    z = z_all[:, bass.ds(ch * CH, CH)]
                    xs = x_all[:, bass.ds(ch * CH, CH), :]
                    own = lin_o[:, b, :, 0:FEAT]
                    conv = lin_o[:, b, :, FEAT:2 * FEAT]
                    dve.wait_ge(s.lin_o, (ch + 1) * CH)
                    if l == 0:
                        link(v.tensor_tensor(cen[:, :, :], own, conv, ALU.add))
                        link(v.tensor_tensor(cen[:, :, :], cen[:, :, :], per_node(z), ALU.mult))
                        link(v.tensor_tensor(squ[:, :, :], cen[:, :, :], xs, ALU.add))
                    else:
                        ang = st[:, 3, :]
                        turns = st[:, 4:6, :]
                        red = st[:, 6:8, :]
                        link(v.tensor_tensor(ang, lin_o[:, b, :, 2 * FEAT], z, ALU.mult))
                        link(v.tensor_scalar(st[:, 4, :], ang, 1.0 / TWO_PI, ROUND, ALU.mult, ALU.add))
                        link(v.tensor_scalar(st[:, 5, :], ang, 1.0 / TWO_PI, 0.25, ALU.mult, ALU.add))
                        link(v.tensor_scalar(st[:, 5, :], st[:, 5, :], ROUND, None, ALU.add))
                        link(v.tensor_scalar(turns, turns, -ROUND, None, ALU.add))
                        ang2 = ang.unsqueeze(1).to_broadcast([P, 2, CH])
                        link(v.scalar_tensor_tensor(red, turns, -PI_A, ang2, ALU.mult, ALU.add))
                        link(v.scalar_tensor_tensor(red, turns, -PI_B, red, ALU.mult, ALU.add))
                        link(v.scalar_tensor_tensor(red, turns, -PI_C, red, ALU.mult, ALU.add))
                        link(v.tensor_scalar(st[:, 7, :], st[:, 7, :], TWO_PI / 4, None, ALU.add))
                        v.tensor_scalar(red, red, 3.1415925, -3.1415925, ALU.min, ALU.max).then_inc(s.ang, 1)
                        dve.wait_ge(s.trig, ch + 1)
                        link(v.tensor_tensor(st[:, 10:12, :], st[:, 8:10, :], z.unsqueeze(1).to_broadcast([P, 2, CH]),
                                             ALU.mult))
                        link(v.tensor_tensor(cen[:, :, :], own, per_node(st[:, 11, :]), ALU.mult))
                        link(v.tensor_tensor(squ[:, :, :], conv, per_node(st[:, 10, :]), ALU.mult))
                        link(v.tensor_tensor(cen[:, :, :], cen[:, :, :], squ[:, :, :], ALU.add))
                        link(v.tensor_tensor(squ[:, :, :], cen[:, :, :], xs, ALU.add))
                    link(v.tensor_reduce(st[:, 0, :], squ[:, :, :], AX_X, ALU.add))
                    link(v.tensor_scalar(st[:, 0, :], st[:, 0, :], 1.0 / FEAT, None, ALU.mult))
                    link(v.tensor_tensor(cen[:, :, :], squ[:, :, :], per_node(st[:, 0, :]), ALU.subtract))
                    link(v.tensor_tensor(squ[:, :, :], cen[:, :, :], cen[:, :, :], ALU.mult))
                    v.tensor_reduce(st[:, 1, :], squ[:, :, :], AX_X, ALU.add).then_inc(s.var, 1)
                    dve.wait_ge(s.root, ch + 1)
                    link(v.reciprocal(st[:, 12, :], st[:, 2, :]))
                    if l == 0:
                        wait(dve, s.stored[b], 16 * it)
                        link(v.tensor_tensor(xs, cen[:, :, :], per_node(st[:, 12, :]), ALU.mult))
                        settle(dve)
                        v.tensor_copy(tab[:, b, :, :], xs).then_inc(s.x, 1)
                    else:
                        wait(dve, s.stored[b], 16 * it)
                        v.tensor_tensor(tab[:, b, :, :], cen[:, :, :], per_node(st[:, 12, :]), ALU.mult).then_inc(s.x, 1)
                    assert c[0] == LINKS, (l, c[0], LINKS)
            loop(dve, body, NCH // 2)

        def node_pool(pool, l):
            s = nodes[l]

            def body(it):
                for b in range(2):
                    ch = 2 * it + b
                    if l == 0:
                        pool.wait_ge(s.xt, (ch + 1) * CH)
                        cols = bass.ds(ch * CH * P, CH * P)
                        settle(pool)
                        pool.dma_start(x1_t[0:S0, cols], xt_s[:, b, :]).then_inc(s.xt_stored[b], 16)
                        pool.dma_start(x1_t[S0:FEAT, cols], xt_v[:, b, :]).then_inc(s.xt_stored[b], 16)
                        pool.wait_ge(s.tab, (ch + 1) * CH)
                        settle(pool)
                        store_table(pool, 1, b, ch, s.stored[b])
                    else:
                        pool.wait_ge(s.x, ch + 1)
                        settle(pool)
                        pool.dma_start(t["out"].rearrange("(n p) f -> p n f", p=P)[:, bass.ds(ch * CH, CH), :],
                                       tab[:, b, :, :]).then_inc(s.stored[b], 16)
            loop(pool, body, NCH // 2)
            for b in range(2):
                pool.wait_ge(s.stored[b], 16 * (NCH // 2))
                if l == 0:
                    pool.wait_ge(s.xt_stored[b], 32 * (NCH // 2))

        def engine_program(eng, setup, tab_step, edge, general, node):
            setup(eng)
            phase_barrier(eng, "setup")
            if tab_step:
                tab_step(eng)
            phase_barrier(eng, "table")
            outside = eng.value_load(flag_i[0:1, 0:1], min_val=0, max_val=1)
            for l in range(2):
                with eng.If(outside == 0):
                    edge(eng, l)
                with eng.Else():
                    general(eng, l)
                phase_barrier(eng, f"edges {l}")
                node(eng, l)
                phase_barrier(eng, f"nodes {l}")

        block = ctx.enter_context(nc.Block())

        @block.sync
        def _(sp):
            engine_program(sp, sp_setup, tab_loads, edge_sp, general_sp, node_sp)

        @block.gpsimd
        def _(pool):
            def setup(pool):
                pool_setup(pool)
                pool.wait_ge(zeroed, 16 * ZERO_DMAS)
            engine_program(pool, setup, tab_pool, edge_pool, general_pool, node_pool)

        @block.scalar
        def _(act):
            engine_program(act, act_setup, tab_act, edge_act, general_act, node_act)

        @block.vector
        def _(dve):
            engine_program(dve, dve_setup, None, edge_dve, general_dve, node_dve)

        @block.tensor
        def _(pe):
            engine_program(pe, pe_setup, tab_pe, edge_pe, general_pe, node_pe)


def kernel(**inputs):
    import numpy as np
    import concourse.bacc as bacc
    from concourse.bass_utils import run_bass_kernel_spmd

    a = {k: np.asarray(v) for k, v in inputs.items()}

    def component_major(v):
        return np.concatenate([v[:, :S0], v[:, S0:].reshape(-1, V0, 3).transpose(0, 2, 1).reshape(-1, 3 * V0)], 1)

    def pad_rows(v, n, mode="constant"):
        return np.pad(v, [(0, n - v.shape[0])] + [(0, 0)] * (v.ndim - 1), mode=mode)

    def weights_of_edges(w):
        return np.concatenate([w[:, :S0], w[:, 2 * S0:2 * S0 + V0], w[:, S0:2 * S0], w[:, 2 * S0 + V0:]], 1)

    def three_blocks(w):
        out = np.zeros((3 * V0, 3 * V0), w.dtype)
        for i in range(3):
            out[i * V0:(i + 1) * V0, i * V0:(i + 1) * V0] = w
        return out

    x = pad_rows(component_major(a["x"]), NPAD)
    EP = T * P
    src = pad_rows(a["src"], EP)
    dst = pad_rows(a["dst"], EP, "edge")
    tiles = dst.reshape(T, P)
    host = {
        "x_rows": x.reshape(NT, P, FEAT).transpose(1, 0, 2),
        "x_t": x.T,
        "z": pad_rows(a["node_vec1"], NPAD).reshape(NT, P).T,
        "src_g": src.reshape(NG, GT, P).transpose(0, 2, 1),
        "src_q": src.reshape(NQ, QT, P).transpose(0, 2, 1),
        "dst_pt": tiles.T,
        "dst_first": dst[::GT * P],
        "dst_flat": dst.reshape(1, EP),
        "y": pad_rows(a["edge_attr_4"], EP).reshape(T, P, 4).transpose(1, 0, 2),
        "attr12_t": pad_rows(a["edge_attr_12"], EP).T,
        "attr8_t": pad_rows(a["edge_attr_8"], EP).T,
        "L0_fc1": a["L0_gnn_W_fc1"], "L0_fc2": weights_of_edges(a["L0_gnn_W_fc2"]),
        "L0_l1_0": a["L0_gnn_W_l1_0"], "L0_l1_1": three_blocks(a["L0_gnn_W_l1_1"]),
        "L0_sc0": a["L0_gnn_W_sc0"], "L0_sc1": three_blocks(a["L0_gnn_W_sc1"]),
        "L0_l2_0": a["L0_gnn_W_l2_0"], "L0_l2_1": a["L0_gnn_W_l2_1"],
        "L1_fc1": a["L1_gnn_fc_w1"], "L1_fc2": weights_of_edges(a["L1_gnn_fc_w2"]),
        "L1_l1_0": a["L1_gnn_lin1_w0"], "L1_l1_1": three_blocks(a["L1_gnn_lin1_w1"]),
        "L1_sc0": a["L1_gnn_sc_w0"], "L1_sc1": three_blocks(a["L1_gnn_sc_w1"]),
        "L1_l2_0": a["L1_gnn_lin2_w0"], "L1_l2_1": a["L1_gnn_lin2_w1"],
        "L1_lin3": a["L1_gnn_lin3_w"],
    }
    nc = bacc.Bacc("TRN2", target_bir_lowering=False, num_devices=1)
    arrays, t = {}, {}
    for name, v in host.items():
        arrays[name] = np.ascontiguousarray(v)
        t[name] = nc.dram_tensor(name, arrays[name].shape, mybir.dt.from_np(arrays[name].dtype), kind="ExternalInput").ap()
    t["out"] = nc.dram_tensor("out", [NPAD, FEAT], F32, kind="ExternalOutput").ap()
    program(nc, t)
    r = run_bass_kernel_spmd(nc, [arrays], core_ids=[0])
    out = r.results[0]["out"][:N]
    return np.concatenate([out[:, :S0], out[:, S0:].reshape(N, 3, V0).transpose(0, 2, 1).reshape(N, 3 * V0)], 1)
```

```python
import math
from contextlib import ExitStack

import concourse.bass as bass
from concourse import mybir

F32 = mybir.dt.float32
BF16 = mybir.dt.bfloat16
I32 = mybir.dt.int32
ALU = mybir.AluOpType
ACT = mybir.ActivationFunctionType
AX_X = mybir.AxisListType.X

P = 128
N = 6250
E = 200000
S0, V0 = 64, 32
FEAT = S0 + 3 * V0
MID = 4 * (S0 + V0)
BLK = S0 + V0
WCOL = 2 * S0 + 2 * V0

QT = 4
GT = 8
NG = 2 * -(-E // (2 * GT * P))
T = NG * GT
NQ = T // QT
ITERS = NG // 2
BODY = 2 * GT * P
AHEAD = 2
NB = ITERS + AHEAD + 1
WIN = 112
HEAD = WIN
HT = NG // 2

CH = 5
NCH = 10
NT = CH * NCH
NPAD = NT * P
TRASH = NPAD - P
assert TRASH >= N and ITERS * 4 == NQ and N + WIN < NPAD and HT <= P


def program(nc, t):
    layers = (
        dict(nef=12, hid=100, attr=t["attr12"], w1=t["L0_fc1"], w2=t["L0_fc2"], fc1_scale=12.0 ** -0.5,
             w2_scale=(100.0 * 8.0) ** -0.5, sc_scale=float(0.3826834323650898),
             conv_scale=float(0.9238795325112867), lin1=(t["L0_l1_0"], t["L0_l1_1"]),
             sc=(t["L0_sc0"], t["L0_sc1"]), lin2=t["L0_l2"], conv_cols=FEAT),
        dict(nef=8, hid=64, attr=t["attr8"], w1=t["L1_fc1"], w2=t["L1_fc2"], fc1_scale=8.0 ** -0.5,
             w2_scale=(64.0 * 16.0) ** -0.5, sc_scale=1.0, conv_scale=1.0,
             lin1=(t["L1_l1_0"], t["L1_l1_1"]), sc=(t["L1_sc0"], t["L1_sc1"]), lin2=t["L1_l2"], conv_cols=FEAT + 1),
    )
    ctx = ExitStack()
    with ctx:
        def sb(name, shape, dt=F32):
            return ctx.enter_context(nc.sbuf_tensor(name, shape, dt))

        def sem(name):
            return ctx.enter_context(nc.semaphore(name))

        table = [nc.dram_tensor(f"table{l}", [NPAD, FEAT], F32, kind="Internal").ap() for l in range(2)]
        acc = [nc.dram_tensor(f"acc{l}", [NPAD, MID], F32, kind="Internal").ap() for l in range(2)]
        heads = [nc.dram_tensor(f"heads{l}", [NG, MID], F32, kind="Internal").ap() for l in range(2)]
        parts = [nc.dram_tensor(f"parts{l}", [2 * NB, 3, layers[l]["nef"], GT * P], BF16, kind="Internal").ap()
                 for l in range(2)]
        x1_t = nc.dram_tensor("x1_t", [FEAT, NPAD], F32, kind="Internal").ap()
        feat_t = (t["x_t"], x1_t)

        src_all = sb("src_all", [P, T], I32)
        y_all = sb("y_all", [P, T, 4])
        dst_f = sb("dst_f", [P, T])
        dst_win = sb("dst_win", [P, T])
        base_f = sb("base_f", [P, NG])
        base_i = sb("base_i", [1, NG], I32)
        base_c = sb("base_c", [HT, 2])
        x_all = sb("x_all", [P, NT, FEAT])
        z_all = sb("z_all", [P, NT])
        ident = sb("ident", [P, P])
        iota_r = sb("iota_r", [P, P])
        iota_p = sb("iota_p", [P, 1])
        below = sb("below", [P, P])
        zeros = sb("zeros", [P, MID])
        eps_col = sb("eps_col", [P, 1])
        w1s = [sb(f"w1s{l}", [layers[l]["nef"], layers[l]["hid"]]) for l in range(2)]
        w1r = [sb(f"w1r{l}", [layers[l]["nef"], 2, layers[l]["hid"]]) for l in range(2)]
        w1p = [sb(f"w1p{l}", [layers[l]["nef"], 3, layers[l]["hid"]], BF16) for l in range(2)]
        w1x = [sb(f"w1x{l}", [9 * layers[l]["nef"], layers[l]["hid"]], BF16) for l in range(2)]
        w2s = [sb(f"w2s{l}", [layers[l]["hid"], WCOL]) for l in range(2)]
        lin1s = [(sb(f"lin1s{l}", [S0, FEAT]), sb(f"lin1v{l}", [3 * V0, FEAT])) for l in range(2)]
        scs = [(sb(f"scs{l}", [S0, FEAT]), sb(f"scv{l}", [3 * V0, FEAT])) for l in range(2)]
        lin2s = [sb(f"lin2s{l}", [P, MID // P, layers[l]["conv_cols"]]) for l in range(2)]
        RAWP = [96, 128]
        RAWX = [BODY * L["nef"] // p for L, p in zip(layers, RAWP)]
        RAWMAX = max(RAWX)
        raw = sb("raw", [P, RAWMAX])
        rest = sb("rest", [P, RAWMAX])
        part = sb("part", [P, 3, RAWMAX], BF16)
        attr = sb("attr_sb", [9 * 12, 2, GT * P], BF16)
        lim = sb("lim", [P, 4])
        lim_r = sb("lim_r", [3, 4])
        flag_f = sb("flag_f", [1, 4])
        flag_i = sb("flag_i", [1, 1], I32)

        WORK = 20200
        work = sb("work", [P, WORK])

        def carve(at, shape):
            size = 1
            for n in shape[1:]:
                size *= n
            assert at[0] + size <= WORK, (at, size)
            v = work[0:shape[0], at[0]:at[0] + size]
            at[0] += size
            names = "abcd"[:len(shape) - 1]
            if len(names) > 1:
                v = v.rearrange(f"p ({' '.join(names)}) -> p {' '.join(names)}", **dict(zip(names[1:], shape[2:])))
            return v

        e = [0]
        gath = carve(e, [P, 2 * GT, FEAT])
        src_i = carve(e, [P, 2, GT]).bitcast(I32)
        hid = carve(e, [100, 2, QT * P])
        wy = carve(e, [P, 2, QT, BLK])
        mul_p = carve(e, [P, QT, S0])
        dot3 = carve(e, [P, QT, 3 * V0]).rearrange("p t (i u) -> p t i u", i=3)
        dot = carve(e, [P, QT, V0])
        msg = carve(e, [P, 2, QT, MID])
        onehot = carve(e, [P, 2, QT, P])
        flush = carve(e, [P, 2, MID])
        head_in = carve(e, [HT, 2, MID])
        attr_g = carve(e, [12, QT * P])
        dst_row = carve(e, [P, QT, P]).bitcast(I32)
        earlier = carve(e, [P, P])
        count = carve(e, [P, QT])
        row_g = carve(e, [P, QT])
        row_gi = [carve(e, [P, 1]).bitcast(I32) for k in range(QT)]
        src_g = carve(e, [P, QT]).bitcast(I32)
        gflush = carve(e, [P, QT, MID])
        n_ = [0]
        mid = carve(n_, [P, 2, CH, MID])
        xt_s = carve(n_, [S0, 2, CH * P])
        xt_v = carve(n_, [3 * V0, 2, CH * P])
        nx_s = carve(n_, [S0, 2, CH * P])
        nx_v = carve(n_, [3 * V0, 2, CH * P])
        mid_t = carve(n_, [P, 2, MID])
        lin_o = carve(n_, [P, 2, CH, 2 * FEAT + 1])
        pre = carve(n_, [P, 2, CH, FEAT])
        xn = carve(n_, [P, 2, CH, FEAT])
        tab = carve(n_, [P, 2, CH, FEAT])
        squ = carve(n_, [P, CH, FEAT])
        st = carve(n_, [P, 2, 32 * CH]).rearrange("p b (s c) -> p b s c", c=CH)
        dst_i = mid.rearrange("p b c m -> p (b c m)")[:, 0:T].bitcast(I32)
        base_bi = pre.rearrange("p b c m -> p (b c m)")[:, 0:NG].bitcast(I32)
        base_ci = xn[0:HT, 0, 0, 0:2].bitcast(I32)
        later = lin_o.rearrange("p b c m -> p (b c m)")[:, 0:T]
        iota_ri = tab[:, 0, 0, 0:P].bitcast(I32)
        iota_pi = tab[:, 0, 1, 0:1].bitcast(I32)

        ps = ctx.enter_context(nc.psum_tensor("ps", [P, 8, 512], F32))

        w_loaded = sem("w_loaded")
        w_turned = sem("w_turned")
        z_loaded = sem("z_loaded")
        dst_loaded = sem("dst_loaded")
        src_loaded = sem("src_loaded")
        y_loaded = sem("y_loaded")
        x_loaded = sem("x_loaded")
        zeros_set = sem("zeros_set")
        zeroed = [sem(f"zeroed{l}") for l in range(2)]
        iota_set = sem("iota_set")
        ident_set = sem("ident_set")
        setup_step = sem("setup_step")
        lim_set = sem("lim_set")
        lim_turned = sem("lim_turned")
        lim_top = sem("lim_top")
        lim_turned2 = sem("lim_turned2")
        w_ready = sem("w_ready")
        part_w = sem("part_w")
        phase_end = sem("phase_end")
        phases = {}

        def phase_barrier(eng):
            phases[eng] = phases.get(eng, 0) + 1
            eng.drain().then_inc(phase_end, 1)
            eng.wait_ge(phase_end, 5 * phases[eng])

        def wait(eng, s, v):
            if isinstance(v, int) and v <= 0:
                return
            eng.wait_ge(s, v)

        passed = {}

        def settle(eng):
            if eng not in passed:
                passed[eng] = sem(f"passed{len(passed)}")
            eng.sem_inc(passed[eng], 1)

        class Sems:
            pass

        def table_sems():
            s = Sems()
            s.xt_in = [sem(f"tab_xt_in{b}") for b in range(2)]
            s.mm = sem("tab_mm")
            s.copied = sem("tab_copied")
            s.stored = [sem(f"tab_stored{b}") for b in range(2)]
            return s

        def edge_sems(l):
            s = Sems()
            s.raw_in = sem(f"l{l}_raw_in")
            s.split = sem(f"l{l}_split")
            s.part_out = sem(f"l{l}_part_out")
            s.attr_in = [sem(f"l{l}_attr_in{b}") for b in range(2)]
            s.rows = sem(f"l{l}_rows")
            s.gathered = [sem(f"l{l}_gathered{k}") for k in range(4)]
            s.fc1 = sem(f"l{l}_fc1")
            s.hid = sem(f"l{l}_hid")
            s.fc2 = sem(f"l{l}_fc2")
            s.wy = sem(f"l{l}_wy")
            s.chain = sem(f"l{l}_chain")
            s.msg = sem(f"l{l}_msg")
            s.seg = sem(f"l{l}_seg")
            s.evac = sem(f"l{l}_evac")
            s.rows_out = sem(f"l{l}_rows_out")
            s.head_out = [sem(f"l{l}_head_out{b}") for b in range(2)]
            s.heads_in = sem(f"l{l}_heads_in")
            s.heads_eq = sem(f"l{l}_heads_eq")
            s.heads_mm = sem(f"l{l}_heads_mm")
            s.heads_sum = sem(f"l{l}_heads_sum")
            s.heads_added = sem(f"l{l}_heads_added")
            return s

        def general_sems(s):
            s.start = s.rows_out
            s.loaded = s.attr_in[0]
            s.added = s.heads_added
            return s

        def node_sems(l):
            s = Sems()
            s.mid_in = [sem(f"l{l}_mid_in{b}") for b in range(2)]
            s.xt_in = [sem(f"l{l}_xt_in{b}") for b in range(2)]
            s.turned = sem(f"l{l}_turned")
            s.mid_t = sem(f"l{l}_mid_t")
            s.lin = sem(f"l{l}_lin")
            s.lin_o = sem(f"l{l}_lin_o")
            s.chain = sem(f"l{l}_node_chain")
            s.pre = sem(f"l{l}_pre")
            s.mean = sem(f"l{l}_mean")
            s.var = sem(f"l{l}_var")
            s.root = sem(f"l{l}_root")
            s.rstd = sem(f"l{l}_rstd")
            s.x = sem(f"l{l}_x")
            s.kept = sem(f"l{l}_kept")
            s.xturn = sem(f"l{l}_xturn")
            s.xt = sem(f"l{l}_xt")
            s.tab_mm = sem(f"l{l}_nt_mm")
            s.tab = sem(f"l{l}_nt_tab")
            s.stored = [sem(f"l{l}_stored{b}") for b in range(2)]
            s.xt_stored = [sem(f"l{l}_xt_stored{b}") for b in range(2)]
            return s

        tabs = table_sems()
        edges = [edge_sems(l) for l in range(2)]
        gens = [general_sems(s) for s in edges]
        nodes = [node_sems(l) for l in range(2)]

        ps_hid = [ps[:, b, :] for b in range(2)]
        ps_w = [ps[:, 2 + 2 * b:4 + 2 * b, :].rearrange("p a c -> p (a c)").rearrange("p (t c) -> p t c", t=QT)
                for b in range(2)]
        ps_acc = [ps[:, 6 + b, 0:MID] for b in range(2)]

        def loop(eng, body, iters, peeled=1):
            for it in range(peeled):
                body(it)
            with eng.Fori(peeled, iters - 1) as it:
                body(it)
            body(iters - 1)

        mult, add, subtract = ALU.mult, ALU.add, ALU.subtract
        v = nc.vector

        WEIGHTS = [(dst, src) for l, L in enumerate(layers) for dst, src in (
            (w1s[l], L["w1"]), (w2s[l], L["w2"]), (lin1s[l][0], L["lin1"][0]), (lin1s[l][1], L["lin1"][1]),
            (scs[l][0], L["sc"][0]), (scs[l][1], L["sc"][1]), (lin2s[l], L["lin2"]))]

        def act_setup(act):
            for dst, src in WEIGHTS:
                act.dma_start(dst[(slice(None),) * len(src.shape)], src).then_inc(w_loaded, 16)

        def sp_setup(sp):
            sp.dma_start(z_all[:, :], t["z"]).then_inc(z_loaded, 16)
            sp.dma_start(dst_i, t["dst_pt"]).then_inc(dst_loaded, 16)
            sp.dma_start(base_bi, t["dst_first"].partition_broadcast(P)).then_inc(dst_loaded, 16)
            sp.dma_start(base_ci, t["dst_first_c"]).then_inc(dst_loaded, 16)
            sp.dma_start(base_i[:, :], t["dst_first"].rearrange("(a g) -> a g", a=1)).then_inc(dst_loaded, 16)

        def pool_setup(pool):
            nc.gpsimd.iota(iota_ri, pattern=[[1, P]], base=0, channel_multiplier=0).then_inc(iota_set, 1)
            nc.gpsimd.iota(iota_pi, pattern=[[0, 1]], base=0, channel_multiplier=1).then_inc(iota_set, 1)
            pool.wait_ge(part_w, 1)
            for l in range(2):
                nef = layers[l]["nef"]
                for j in range(3):
                    for i in range(3):
                        r = (3 * j + i) * nef
                        pool.dma_start(w1x[l][r:r + nef, :], w1p[l][:, j, :]).then_inc(w_turned, 16)

        steps = [0]

        def dve_link(dve):
            def link(ins):
                steps[0] += 1
                ins.then_inc(setup_step, 1)
                dve.wait_ge(setup_step, steps[0])
            return link

        def dve_constants(dve):
            link = dve_link(dve)

            v.memset(zeros[:, :], 0.0).then_inc(zeros_set, 1)
            v.memset(eps_col[:, :], 1e-5)
            dve.wait_ge(iota_set, 2)
            v.tensor_copy(iota_r[:, :], iota_ri)
            link(v.tensor_copy(iota_p[:, :], iota_pi))
            v.tensor_scalar(ident[:, :], iota_r[:, :], iota_p[:, 0:1], None, ALU.is_equal).then_inc(ident_set, 1)
            v.tensor_scalar(below[:, :], iota_r[:, :], iota_p[:, 0:1], None, ALU.is_lt)

        def dve_weights(dve):
            link = dve_link(dve)
            dve.wait_ge(w_loaded, 16 * len(WEIGHTS))
            for l, L in enumerate(layers):
                for (ws, wv), k in ((lin1s[l], 1.0), (scs[l], L["sc_scale"])):
                    v.tensor_scalar(ws[:, :], ws[:, :], k * S0 ** -0.5, None, mult)
                    v.tensor_scalar(wv[:, :], wv[:, :], k * V0 ** -0.5, None, mult)
                v.tensor_scalar(lin2s[l][:, :, 0:FEAT], lin2s[l][:, :, 0:FEAT], L["conv_scale"] * BLK ** -0.5,
                                None, mult)
                link(v.tensor_scalar(w2s[l][:, :], w2s[l][:, :], L["w2_scale"], None, mult))
                v.tensor_scalar(w2s[l][:, WCOL - V0:WCOL], w2s[l][:, WCOL - V0:WCOL], 3.0 ** -0.5, None, mult)
                link(v.tensor_copy(w1p[l][:, 0, :], w1s[l][:, :]))
                link(v.tensor_tensor(w1r[l][:, 0, :], w1s[l][:, :], w1p[l][:, 0, :], subtract))
                link(v.tensor_copy(w1p[l][:, 1, :], w1r[l][:, 0, :]))
                ins = v.tensor_tensor(w1p[l][:, 2, :], w1r[l][:, 0, :], w1p[l][:, 1, :], subtract)
                if l == 0:
                    link(ins)
                else:
                    ins.then_inc(part_w, 1)
            v.tensor_scalar(lin2s[1][:, :, FEAT:FEAT + 1], lin2s[1][:, :, FEAT:FEAT + 1], 0.1 * BLK ** -0.5, None,
                            mult).then_inc(w_ready, 1)

        def dve_windows(dve):
            link = dve_link(dve)

            def by_group(a):
                return a.rearrange("p (g k) -> p g k", k=GT)

            dve.wait_ge(dst_loaded, 16 * 4)
            v.tensor_copy(dst_f[:, :], dst_i)
            v.tensor_copy(base_c[:, :], base_ci)
            link(v.tensor_copy(base_f[:, :], base_bi))
            link(v.tensor_tensor(by_group(dst_win[:, :]), by_group(dst_f[:, :]),
                                 base_f[:, :].unsqueeze(2).to_broadcast([P, NG, GT]), subtract))
            v.tensor_reduce(lim[:, 0:1], dst_win[:, :], AX_X, ALU.max)
            v.tensor_reduce(lim[:, 1:2], dst_win[:, :], AX_X, ALU.min)
            G1 = NG - 1
            link(v.tensor_tensor(by_group(later)[:, 0:G1, :], by_group(dst_f[:, :])[:, 0:G1, :],
                                 base_f[:, 1:NG].unsqueeze(2).to_broadcast([P, G1, GT]), subtract))
            link(v.tensor_reduce(lim[:, 2:3], later[:, 0:G1 * GT], AX_X, ALU.max))
            v.tensor_scalar(lim[:, 2:3], lim[:, 2:3], float(WIN), None, add)
            v.tensor_scalar(lim[:, 1:2], lim[:, 1:2], -1.0, float(WIN), mult, add).then_inc(lim_set, 1)
            link(v.tensor_scalar(later, dst_win[:, :], 0.0, float(WIN + 1), ALU.is_equal, mult))
            link(v.tensor_scalar(later, later, -1.0, None, add))
            link(v.tensor_tensor(dst_win[:, :], dst_win[:, :], later, add))
            dve.wait_ge(lim_turned, 1)
            v.tensor_reduce(lim_r[:, 0:1], ps[0:3, 4, 0:P], AX_X, ALU.max).then_inc(lim_top, 1)
            dve.wait_ge(lim_turned2, 1)
            v.tensor_reduce(flag_f[:, 0:1], ps[0:1, 5, 0:3], AX_X, ALU.max)
            link(v.tensor_reduce(flag_f[:, 1:2], base_f[0:1, :], AX_X, ALU.max))
            link(v.tensor_scalar(flag_f[:, 1:2], flag_f[:, 1:2], float(N), None, ALU.is_ge))
            link(v.tensor_scalar(flag_f[:, 0:1], flag_f[:, 0:1], float(WIN), None, ALU.is_gt))
            link(v.tensor_tensor(flag_f[:, 2:3], flag_f[:, 0:1], flag_f[:, 1:2], ALU.max))
            v.tensor_copy(flag_i[:, :], flag_f[:, 2:3])

        def pe_windows(pe):
            pe.wait_ge(ident_set, 1)
            pe.wait_ge(lim_set, 1)
            nc.tensor.transpose(ps[0:3, 4, 0:P], lim[:, 0:3], ident[:, :]).then_inc(lim_turned, 1)
            pe.wait_ge(lim_top, 1)
            nc.tensor.transpose(ps[0:1, 5, 0:3], lim_r[:, 0:1], ident[0:3, 0:3]).then_inc(lim_turned2, 1)

        def zero_rows(sp, l, ch):
            sp.dma_start(acc[l].rearrange("(n p) m -> p n m", p=P)[:, bass.ds(ch * CH, CH), :],
                         zeros[:, :].unsqueeze(1).to_broadcast([P, CH, MID])).then_inc(zeroed[l], 16)

        def tab_loads(sp):
            def body(it):
                for b in range(2):
                    wait(sp, tabs.mm, (2 * it + b - 1) * CH)
                    settle(sp)
                    cols = bass.ds((2 * it + b) * CH * P, CH * P)
                    sp.dma_start(xt_s[:, b, :], feat_t[0][0:S0, cols]).then_inc(tabs.xt_in[b], 16)
                    sp.dma_start(xt_v[:, b, :], feat_t[0][S0:FEAT, cols]).then_inc(tabs.xt_in[b], 16)
                    zero_rows(sp, 0, 2 * it + b)
            for l in (1, 0):
                split_first(sp, l, "sp")
            sp.wait_ge(zeros_set, 1)
            loop(sp, body, NCH // 2)
            sp.dma_start(src_all[:, :], t["src_pt"]).then_inc(src_loaded, 16)
            sp.dma_start(y_all[:, :, :], t["y"]).then_inc(y_loaded, 16)
            sp.dma_start(x_all[:, :, :], t["x_rows"]).then_inc(x_loaded, 16)

        def table_mm(out, xs, xv, l, b, i):
            c = slice(i * P, (i + 1) * P)
            nc.tensor.matmul(out[:, 0:FEAT], xs[:, b, c], lin1s[l][0][:, :], start=True, stop=False)
            return nc.tensor.matmul(out[:, 0:FEAT], xv[:, b, c], lin1s[l][1][:, :], start=False, stop=True)

        def tab_pe(pe):
            pe.wait_ge(w_ready, 1)

            def body(it):
                for b in range(2):
                    pe.wait_ge(tabs.xt_in[b], 32 * (it + 1))
                    for i in range(CH):
                        n = (2 * it + b) * CH + i
                        k = b * CH + i
                        wait(pe, tabs.copied, n - 1)
                        table_mm(ps[:, 6 + k % 2, :], xt_s, xt_v, 0, b, i).then_inc(tabs.mm, 1)
            loop(pe, body, NCH // 2)

        def tab_act(act):
            act.wait_ge(z_loaded, 16)

            def body(it):
                for b in range(2):
                    wait(act, tabs.stored[b], 16 * it)
                    for i in range(CH):
                        n = (2 * it + b) * CH + i
                        k = b * CH + i
                        act.wait_ge(tabs.mm, n + 1)
                        nc.scalar.activation(tab[:, b, i, :], ps[:, 6 + k % 2, 0:FEAT], ACT.Copy,
                                             scale=z_all[:, bass.ds(n, 1)]).then_inc(tabs.copied, 1)
            loop(act, body, NCH // 2)

        def store_table(eng, l, b, ch, done):
            eng.dma_start(table[l].rearrange("(n p) f -> p n f", p=P)[:, bass.ds(ch * CH, CH), :],
                          tab[:, b, :, :]).then_inc(done, 16)

        def tab_pool(pool):
            def body(it):
                for b in range(2):
                    pool.wait_ge(tabs.copied, (2 * it + b + 1) * CH)
                    settle(pool)
                    store_table(pool, 0, b, 2 * it + b, tabs.stored[b])
            loop(pool, body, NCH // 2)
            for b in range(2):
                pool.wait_ge(tabs.stored[b], 16 * (NCH // 2))

        def raw_load(sp, l, n):
            s, L = edges[l], layers[l]
            sp.dma_start(raw[0:RAWP[l], 0:RAWX[l]],
                         L["attr"][bass.ds(n * 2, 2), :, :].rearrange("g f c -> (g f c)")
                         .rearrange("(p x) -> p x", p=RAWP[l])).then_inc(s.raw_in, 16)

        def part_store(sp, l, n):
            s, h = edges[l], RAWP[l] // 2
            for i in range(3):
                for b in range(2):
                    sp.dma_start(parts[l][bass.ds(n * 2 + b, 1), i, :, :].rearrange("g f c -> (g f c)")
                                 .rearrange("(p x) -> p x", p=h),
                                 part[b * h:(b + 1) * h, i, 0:RAWX[l]]).then_inc(s.part_out, 16)

        PARTS_INC = 16 * 6

        def attr_load(sp, l, n, b):
            s, rows = edges[l], 3 * layers[l]["nef"]
            for j in range(3):
                sp.dma_start(attr[j * rows:(j + 1) * rows, b, :],
                             parts[l][bass.ds(n * 2 + b, 1), :, :, :].rearrange("g i f c -> (g i f) c")
                             ).then_inc(s.attr_in[b], 16)

        ATTR_INC = 16 * 3

        def split_copy(act, l, n, i):
            s, p, x = edges[l], RAWP[l], RAWX[l]
            if i == 0:
                act.wait_ge(s.raw_in, 16 * (n + 1))
                wait(act, s.part_out, PARTS_INC * n)
            else:
                act.wait_ge(s.split, 4 * n + 2)
            nc.scalar.activation(part[0:p, i, 0:x], (rest if i else raw)[0:p, 0:x], ACT.Copy).then_inc(s.split, 1)

        def split_rest(dve, l, n, i):
            s, p, x = edges[l], RAWP[l], RAWX[l]
            dve.wait_ge(s.split, 4 * n + 2 * i + 1)
            if i == 0:
                v.tensor_tensor(rest[0:p, 0:x], raw[0:p, 0:x], part[0:p, 0, 0:x], subtract).then_inc(s.split, 1)
            else:
                v.tensor_tensor(part[0:p, 2, 0:x], rest[0:p, 0:x], part[0:p, 1, 0:x], subtract).then_inc(s.split, 1)

        def split_first(eng, l, role):
            s = edges[l]
            if l == 0 and role == "sp":
                eng.wait_ge(edges[1].split, 4 * AHEAD)
            if l == 0 and role == "act":
                eng.wait_ge(edges[1].part_out, PARTS_INC * AHEAD)
            for n in range(AHEAD):
                if role == "sp":
                    wait(eng, s.split, 4 * n)
                    raw_load(eng, l, n)
                    eng.wait_ge(s.split, 4 * (n + 1))
                    part_store(eng, l, n)
                elif role == "act":
                    for i in range(2):
                        split_copy(eng, l, n, i)
                elif role == "dve":
                    for i in range(2):
                        split_rest(eng, l, n, i)

        def edge_sp(sp, l):
            s = edges[l]

            raw_load(sp, l, AHEAD)
            sp.wait_ge(s.part_out, PARTS_INC)
            for b in range(2):
                attr_load(sp, l, 0, b)
            sp.wait_ge(zeroed[l], 16 * NCH)

            def sums_store(g, b):
                base = sp.value_load(base_i[0:1, bass.ds(g, 1)], min_val=0, max_val=N - 1)
                sp.wait_ge(s.evac, g + 1)
                settle(sp)
                wait(sp, s.rows_out, 16 * g)
                settle(sp)
                sp.dma_start(acc[l][bass.ds(base + 1, WIN), :], flush[0:WIN, b, :]).then_inc(s.rows_out, 16)
                sp.dma_start(heads[l][bass.ds(g, 1), :], flush[HEAD:HEAD + 1, b, :]).then_inc(s.head_out[b], 16)

            def next_attr(it, b):
                sp.wait_ge(s.part_out, PARTS_INC * (it + 2))
                settle(sp)
                sp.wait_ge(s.fc1, 4 * it + 2 * b + 2)
                settle(sp)
                attr_load(sp, l, it + 1, b)

            def body(it):
                last = isinstance(it, int) and it == ITERS - 1
                if not (isinstance(it, int) and it == 0):
                    sums_store(2 * it - 1, 1)
                if not last:
                    next_attr(it, 0)
                sp.wait_ge(s.split, 4 * (it + AHEAD + 1))
                settle(sp)
                part_store(sp, l, it + AHEAD)
                if not last:
                    raw_load(sp, l, it + AHEAD + 1)
                sums_store(2 * it, 0)
                if not last:
                    next_attr(it, 1)
            loop(sp, body, ITERS)
            sums_store(NG - 1, 1)
            for b in range(2):
                sp.wait_ge(s.head_out[b], 16 * ITERS)
            sp.wait_ge(s.rows_out, 16 * NG)
            sp.wait_ge(s.part_out, PARTS_INC * (ITERS + AHEAD))
            sp.dma_start(head_in, heads[l].rearrange("(c p) m -> p c m", p=HT)).then_inc(s.heads_in, 16)

        def edge_pool(pool, l):
            s = edges[l]

            def rows_copy(g, b):
                nc.gpsimd.tensor_copy(src_i[:, b, :], src_all[:, bass.ds(g * GT, GT)]).then_inc(s.rows, 1)

            if l == 0:
                pool.wait_ge(src_loaded, 16)
            rows_copy(0, 0)

            def body(it):
                for b in range(2):
                    g = 2 * it + b
                    pool.wait_ge(s.rows, g + 1)
                    for k in range(GT):
                        if k == QT and not (isinstance(it, int) and g + 1 == NG):
                            for q in range(2):
                                wait(pool, s.gathered[2 * (1 - b) + q], 16 * QT * (it + b))
                            settle(pool)
                            rows_copy(g + 1, 1 - b)
                        if k % QT == 0:
                            wait(pool, s.msg, 4 * it + 2 * b + k // QT - 3)
                            settle(pool)
                        pool.indirect_dma_start(gath[:, GT * b + k, :], None, table[l],
                                                bass.IndirectOffsetOnAxis(ap=src_i[:, b, k:k + 1], axis=0)
                                                ).then_inc(s.gathered[2 * b + k // QT], 16)
            loop(pool, body, ITERS)
            for c in range(2):
                pool.wait_ge(s.heads_sum, c + 1)
                pool.indirect_dma_start(acc[l], bass.IndirectOffsetOnAxis(ap=row_gi[c][0:HT, :], axis=0),
                                        gflush[0:HT, c, :], None, compute_op=add).then_inc(s.heads_added, 16)
                pool.wait_ge(s.heads_added, 16 * (c + 1))

        def fc2_mm(L, l, b):
            for k in range(QT):
                ins = nc.tensor.matmul(ps_w[b][:, k, 0:WCOL], hid[0:L["hid"], b, k * P:(k + 1) * P], w2s[l][:, :],
                                       start=True, stop=True)
            return ins

        def edge_pe(pe, l):
            s, L = edges[l], layers[l]
            rows = 9 * L["nef"]
            pe.wait_ge(w_turned, 16 * 18)

            def fc1(k, j, it):
                b = (j // 2) % 2
                if j % 2 == 0:
                    pe.wait_ge(s.attr_in[b], ATTR_INC * (it + j // 4 + 1))
                wait(pe, s.hid, k - 1)
                nc.tensor.matmul(ps_hid[j % 2][0:L["hid"], :], w1x[l][:, :],
                                 attr[0:rows, b, (j % 2) * QT * P:(j % 2 + 1) * QT * P], start=True, stop=True
                                 ).then_inc(s.fc1, 1)

            def fc2(k, j):
                pe.wait_ge(s.hid, k + 1)
                wait(pe, s.msg, k - 1)
                fc2_mm(L, l, j % 2).then_inc(s.fc2, 1)

            fc1(0, 0, 0)
            fc1(1, 1, 0)
            fc2(0, 0)

            def body(it):
                for j in range(4):
                    k = 4 * it + j
                    if not (isinstance(it, int) and k + 2 >= NQ):
                        fc1(k + 2, j + 2, it)
                    if not (isinstance(it, int) and k + 1 >= NQ):
                        fc2(k + 1, j + 1)
                    g = 2 * it + j // 2
                    if j % 2 == 0:
                        wait(pe, s.evac, g - 1)
                    pe.wait_ge(s.msg, k + 1)
                    for q in range(QT):
                        ins = nc.tensor.matmul(ps_acc[j // 2], onehot[:, j % 2, q, :], msg[:, j % 2, q, :],
                                               start=(j % 2 == 0 and q == 0), stop=(j % 2 == 1 and q == QT - 1))
                    ins.then_inc(s.seg, 1)
            loop(pe, body, ITERS)
            pe.wait_ge(s.heads_eq, 1)
            pe.wait_ge(s.heads_in, 16)
            for c in range(2):
                ins = nc.tensor.matmul(ps[0:HT, c, 0:MID], onehot[0:HT, 0, c, 0:HT], head_in[:, c, :],
                                       start=True, stop=True)
            ins.then_inc(s.heads_mm, 1)

        def silu(L, b):
            return nc.scalar.activation(hid[0:L["hid"], b, :], ps_hid[b][0:L["hid"], :], ACT.Silu,
                                        scale=L["fc1_scale"])

        def wy_copy(b, tile0):
            for k in range(QT):
                ins = nc.scalar.activation(wy[:, b, k, :], ps_w[b][:, k, 0:BLK], ACT.Copy,
                                           scale=y_all[:, bass.ds(tile0 + k, 1), 0:1].rearrange("p a b -> p (a b)"))
            return ins

        def edge_act(act, l):
            s, L = edges[l], layers[l]
            if l == 0:
                act.wait_ge(y_loaded, 16)

            def hidden(k, j):
                act.wait_ge(s.fc1, k + 1)
                wait(act, s.fc2, k - 1)
                silu(L, j % 2).then_inc(s.hid, 1)

            def weights(k, j):
                act.wait_ge(s.fc2, k + 1)
                wait(act, s.msg, k - 1)
                wy_copy(j % 2, k * QT).then_inc(s.wy, 1)

            hidden(0, 0)
            hidden(1, 1)
            weights(0, 0)

            def body(it):
                for j in range(4):
                    k = 4 * it + j
                    if not (isinstance(it, int) and k + 2 >= NQ):
                        hidden(k + 2, j)
                    if j < 2:
                        split_copy(act, l, it + AHEAD, j)
                    if not (isinstance(it, int) and k + 1 >= NQ):
                        weights(k + 1, j + 1)
                    if j % 2 == 1:
                        b = j // 2
                        wait(act, s.head_out[b], 16 * it)
                        wait(act, s.rows_out, 16 * (2 * it + b - 1))
                        act.wait_ge(s.seg, k + 1)
                        nc.scalar.activation(flush[:, b, :], ps_acc[b], ACT.Copy).then_inc(s.evac, 1)
            loop(act, body, ITERS)
            act.wait_ge(s.heads_mm, 1)
            for c in range(2):
                nc.scalar.activation(row_gi[c][0:HT, :], row_g[0:HT, c:c + 1], ACT.Copy)
                nc.scalar.activation(gflush[0:HT, c, :], ps[0:HT, c, 0:MID], ACT.Copy).then_inc(s.heads_sum, 1)

        def messages(dve, s, k, chain, wait_chain, b, g, tile0):
            h0 = g[:, :, 0:S0]
            h1 = g[:, :, S0:FEAT].rearrange("p t (i u) -> p t i u", i=3)
            yv = y_all[:, bass.ds(tile0, QT), 1:4]
            w = ps_w[b]
            m = msg[:, b, :, :].rearrange("p t (a c) -> p t a c", a=4)
            v.tensor_tensor(dot3, h1, yv.unsqueeze(3).to_broadcast([P, QT, 3, V0]), mult).then_inc(chain, 1)
            wait_chain(1)
            v.tensor_tensor(dot, dot3[:, :, 0, :], dot3[:, :, 1, :], add).then_inc(chain, 1)
            wait_chain(2)
            v.tensor_tensor(dot, dot, dot3[:, :, 2, :], add).then_inc(chain, 1)
            dve.wait_ge(s.wy, k + 1)
            v.tensor_tensor(mul_p, w[:, :, BLK:BLK + S0], h0, mult).then_inc(chain, 1)
            v.tensor_tensor(m[:, :, 0, 0:S0], wy[:, b, :, 0:S0], h0, mult)
            wait_chain(4)
            v.tensor_tensor(m[:, :, 1:4, 0:S0], mul_p.unsqueeze(2).to_broadcast([P, QT, 3, S0]),
                            yv.unsqueeze(3).to_broadcast([P, QT, 3, S0]), mult)
            v.tensor_tensor(m[:, :, 1:4, S0:BLK], wy[:, b, :, S0:BLK].unsqueeze(2).to_broadcast([P, QT, 3, V0]),
                            h1, mult)
            return v.tensor_tensor(m[:, :, 0, S0:BLK], w[:, :, BLK + S0:WCOL], dot, mult)

        def edge_dve(dve, l):
            s = edges[l]
            if l == 0:
                dve.wait_ge(y_loaded, 16)

            def body(it):
                for j in range(4):
                    k = 4 * it + j
                    wait(dve, s.seg, k - 1)
                    v.tensor_tensor(
                        onehot[:, j % 2, :, :], iota_r[:, :].unsqueeze(1).to_broadcast([P, QT, P]),
                        dst_win[:, bass.ds(k * QT, QT)].unsqueeze(2).to_broadcast([P, QT, P]), ALU.is_equal)
                    dve.wait_ge(s.gathered[j], 16 * QT * (it + 1))
                    messages(dve, s, k, s.chain, lambda n: dve.wait_ge(s.chain, k * 4 + n), j % 2,
                             gath[:, QT * j:QT * (j + 1), :], k * QT).then_inc(s.msg, 1)
                    if j < 2:
                        split_rest(dve, l, it + AHEAD, j)
            loop(dve, body, ITERS)
            c = [4 * NQ]

            def link(ins):
                c[0] += 1
                ins.then_inc(s.chain, 1)
                dve.wait_ge(s.chain, c[0])

            dve.wait_ge(s.seg, NQ)
            for h in range(2):
                link(v.tensor_scalar(onehot[0:HT, 0, h, 0:HT], base_f[0:HT, h * HT:(h + 1) * HT],
                                     base_c[:, h:h + 1], None, ALU.is_equal))
                link(v.tensor_tensor(earlier[0:HT, 0:HT], onehot[0:HT, 0, h, 0:HT], below[0:HT, 0:HT], mult))
                link(v.tensor_reduce(count[0:HT, h:h + 1], earlier[0:HT, 0:HT], AX_X, ALU.max))
            pick_rows(link, HT, 2, base_c[:, :]).then_inc(s.heads_eq, 1)

        def pick_rows(link, rows, n, dst):
            r, k = row_g[0:rows, 0:n], count[0:rows, 0:n]
            link(v.tensor_tensor(r, iota_p[0:rows, 0:1].to_broadcast([rows, n]), dst, subtract))
            link(v.tensor_scalar(r, r, float(TRASH), None, add))
            link(v.tensor_tensor(r, r, k, mult))
            return v.tensor_tensor(r, r, dst, add)

        def general_sp(sp, l):
            s, L = gens[l], layers[l]
            sp.wait_ge(zeroed[l], 16 * NCH)
            sp.wait_ge(edges[l].part_out, PARTS_INC * AHEAD)
            with sp.Fori(0, NG) as g:
                for h in range(2):
                    k = 2 * g + h
                    sp.wait_ge(s.start, k + 1)
                    settle(sp)
                    sp.dma_start(attr_g[0:L["nef"], :], L["attr"][bass.ds(g, 1), :, h * QT * P:(h + 1) * QT * P]
                                 .rearrange("g f c -> (g f) c")).then_inc(s.loaded, 16)
                    sp.dma_start(src_g, t["src_pt"][:, bass.ds(k * QT, QT)]).then_inc(s.loaded, 16)
                    sp.dma_start(dst_row.rearrange("p t e -> p (t e)"),
                                 t["dst_flat"][:, bass.ds(k * QT * P, QT * P)].rearrange("a e -> (a e)")
                                 .partition_broadcast(P)).then_inc(s.loaded, 16)

        def general_pool(pool, l):
            s = gens[l]
            pool.sem_inc(s.start, 1)
            with pool.Fori(0, NQ) as k:
                pool.wait_ge(s.loaded, 48 * (k + 1))
                settle(pool)
                for q in range(QT):
                    pool.indirect_dma_start(gath[:, q, :], None, table[l],
                                            bass.IndirectOffsetOnAxis(ap=src_g[:, q:q + 1], axis=0)
                                            ).then_inc(s.gathered[0], 16)
                pool.wait_ge(s.evac, k + 1)
                settle(pool)
                for q in range(QT):
                    pool.indirect_dma_start(acc[l], bass.IndirectOffsetOnAxis(ap=row_gi[q], axis=0),
                                            gflush[:, q, :], None, compute_op=add).then_inc(s.added, 16)
                    pool.wait_ge(s.added, 16 * (k * QT + q + 1))
                    settle(pool)
                pool.sem_inc(s.start, 1)

        def general_pe(pe, l):
            s, L = gens[l], layers[l]
            with pe.Fori(0, NQ) as k:
                pe.wait_ge(s.loaded, 48 * (k + 1))
                nc.tensor.matmul(ps_hid[0][0:L["hid"], :], w1s[l][:, :], attr_g[0:L["nef"], :], start=True, stop=True
                                 ).then_inc(s.fc1, 1)
                pe.wait_ge(s.hid, k + 1)
                fc2_mm(L, l, 0).then_inc(s.fc2, 1)
                pe.wait_ge(s.msg, k + 1)
                for q in range(QT):
                    ins = nc.tensor.matmul(ps[:, 4 + q, 0:MID], onehot[:, 0, q, :], msg[:, 0, q, :],
                                           start=True, stop=True)
                ins.then_inc(s.seg, 1)

        def general_act(act, l):
            s, L = gens[l], layers[l]
            if l == 0:
                act.wait_ge(y_loaded, 16)
            with act.Fori(0, NQ) as k:
                act.wait_ge(s.fc1, k + 1)
                silu(L, 0).then_inc(s.hid, 1)
                act.wait_ge(s.fc2, k + 1)
                wy_copy(0, k * QT).then_inc(s.wy, 1)
                act.wait_ge(s.seg, k + 1)
                for q in range(QT):
                    nc.scalar.activation(row_gi[q], row_g[:, q:q + 1], ACT.Copy)
                nc.scalar.activation(gflush, ps[:, 4:4 + QT, 0:MID], ACT.Copy).then_inc(s.evac, 1)

        def general_dve(dve, l):
            s = gens[l]
            LINKS = 4 + 3 * QT + 2 + 3
            if l == 0:
                dve.wait_ge(y_loaded, 16)
            with dve.Fori(0, NQ) as k:
                c = [4]

                def link(ins):
                    c[0] += 1
                    ins.then_inc(s.chain, 1)
                    dve.wait_ge(s.chain, k * LINKS + c[0])

                dve.wait_ge(s.loaded, 48 * (k + 1))
                dve.wait_ge(s.gathered[0], 16 * QT * (k + 1))
                messages(dve, s, k, s.chain, lambda n: dve.wait_ge(s.chain, k * LINKS + n), 0, gath[:, 0:QT, :], k * QT)
                dst_q = dst_f[:, bass.ds(k * QT, QT)]
                for q in range(QT):
                    link(v.tensor_tensor(onehot[:, 0, q, :], dst_row[:, q, :],
                                         dst_f[:, bass.ds(k * QT + q, 1)].to_broadcast([P, P]), ALU.is_equal))
                    link(v.tensor_tensor(earlier, onehot[:, 0, q, :], below[:, :], mult))
                    link(v.tensor_reduce(count[:, q:q + 1], earlier, AX_X, ALU.max))
                link(v.tensor_scalar(row_g, dst_q, float(N), None, ALU.is_ge))
                link(v.tensor_tensor(count, count, row_g, ALU.max))
                pick_rows(link, P, QT, dst_q).then_inc(s.msg, 1)
                assert c[0] == LINKS

        def node_sp(sp, l):
            s = nodes[l]

            def body(it):
                for b in range(2):
                    ch = 2 * it + b
                    if l == 0:
                        zero_rows(sp, 1, ch)
                    wait(sp, s.turned, (ch - 1) * CH)
                    settle(sp)
                    sp.dma_start(mid[:, b, :, :], acc[l].rearrange("(n p) m -> p n m", p=P)[:, bass.ds(ch * CH, CH), :]
                                 ).then_inc(s.mid_in[b], 16)
                    wait(sp, s.lin, (ch - 1) * CH)
                    settle(sp)
                    cols = bass.ds(ch * CH * P, CH * P)
                    sp.dma_start(xt_s[:, b, :], feat_t[l][0:S0, cols]).then_inc(s.xt_in[b], 16)
                    sp.dma_start(xt_v[:, b, :], feat_t[l][S0:FEAT, cols]).then_inc(s.xt_in[b], 16)
            loop(sp, body, NCH // 2)

        def run_chunks(eng, body, finish=None, tail=None):
            def step(it):
                for b in range(2):
                    body(2 * it + b, it, b)
                    if finish and not (isinstance(it, int) and it == 0 and b == 0):
                        finish(2 * it + b - 1, it if b else it - 1, 1 - b)
            loop(eng, step, NCH // 2, peeled=2)
            if finish:
                finish(NCH - 1, NCH // 2 - 1, 1)
            if tail:
                for b in range(2):
                    tail(NCH - 2 + b, NCH // 2 - 1, b)

        def node_pe(pe, l):
            s = nodes[l]

            def front(ch, it, b):
                pe.wait_ge(s.mid_in[b], 16 * (it + 1))
                pe.wait_ge(s.xt_in[b], 32 * (it + 1))

                def turn(i):
                    n, k = ch * CH + i, (b * CH + i) % 2
                    wait(pe, s.mid_t, n - 1)
                    for q in range(MID // P):
                        ins = nc.tensor.transpose(ps[:, k, q * P:(q + 1) * P], mid[:, b, i, q * P:(q + 1) * P],
                                                  ident[:, :])
                    ins.then_inc(s.turned, 1)

                def lin(i):
                    n, k = ch * CH + i, (b * CH + i) % 2
                    c = slice(i * P, (i + 1) * P)
                    o = ps[:, 2 + k, :]
                    wait(pe, s.pre if l == 0 else s.lin_o, n - 1)
                    nc.tensor.matmul(o[:, 0:FEAT], xt_s[:, b, c], scs[l][0][:, :], start=True, stop=False)
                    nc.tensor.matmul(o[:, 0:FEAT], xt_v[:, b, c], scs[l][1][:, :], start=False, stop=l == 1)
                    pe.wait_ge(s.mid_t, n + 1)
                    at, cols = 0 if l == 0 else FEAT, layers[l]["conv_cols"]
                    for q in range(MID // P):
                        ins = nc.tensor.matmul(o[:, at:at + cols], mid_t[:, k, q * P:(q + 1) * P], lin2s[l][:, q, :],
                                               start=l == 1 and q == 0, stop=q == MID // P - 1)
                    ins.then_inc(s.lin, 1)

                behind = l == 0 and not (isinstance(it, int) and it == 0)
                turn(0)
                for i in range(CH):
                    if i + 1 < CH:
                        turn(i + 1)
                    lin(i)
                    if behind:
                        tail_turn(ch - 2, b, i)
                        if i > 0:
                            tail_mm(ch - 2, b, i - 1)
                if behind:
                    tail_mm(ch - 2, b, CH - 1)

            def tail_turn(ch, b, i):
                n, k = ch * CH + i, (b * CH + i) % 2
                if i == 0:
                    pe.wait_ge(s.x, ch + 1)
                wait(pe, s.xt, n - 1)
                settle(pe)
                nc.tensor.transpose(ps[0:S0, 4 + k, 0:P], xn[:, b, i, 0:S0], ident[:, :])
                nc.tensor.transpose(ps[0:3 * V0, 4 + k, P:2 * P], xn[:, b, i, S0:FEAT], ident[:, :]
                                    ).then_inc(s.xturn, 1)

            def tail_mm(ch, b, i):
                n, k = ch * CH + i, (b * CH + i) % 2
                pe.wait_ge(s.xt, n + 1)
                wait(pe, s.tab, n - 1)
                table_mm(ps[:, 6 + k, :], nx_s, nx_v, 1, b, i).then_inc(s.tab_mm, 1)

            def tail(ch, it, b):
                for i in range(CH):
                    tail_turn(ch, b, i)
                    if i > 0:
                        tail_mm(ch, b, i - 1)
                tail_mm(ch, b, CH - 1)

            run_chunks(pe, front, tail=tail if l == 0 else None)

        def mid_copy(eng, s, n, k, fn):
            eng.wait_ge(s.turned, n + 1)
            wait(eng, s.lin, n - 1)
            fn(mid_t[:, k, :], ps[:, k, 0:MID]).then_inc(s.mid_t, 1)

        def node_act(act, l):
            s = nodes[l]

            def evac(ch, b, i):
                n, k = ch * CH + i, (b * CH + i) % 2
                act.wait_ge(s.lin, n + 1)
                if i == 0:
                    wait(act, s.pre, (ch - 1) * CH)
                nc.scalar.activation(lin_o[:, b, i, :], ps[:, 2 + k, 0:2 * FEAT + 1], ACT.Copy).then_inc(s.lin_o, 1)

            def front1(ch, it, b):
                for i in range(CH):
                    n, k = ch * CH + i, (b * CH + i) % 2
                    mid_copy(act, s, n, k, lambda o, x: nc.scalar.activation(o, x, ACT.Copy))
                    if i > 0:
                        evac(ch, b, i - 1)
                evac(ch, b, CH - 1)

            def stats(ch, it, b):
                act.wait_ge(s.mean, ch + 1)
                for i in range(CH):
                    ins = nc.scalar.activation(squ[:, i, :], pre[:, b, i, :], ACT.Square, bias=st[:, b, 1, i:i + 1],
                                               accum_out=st[:, b, 2, i:i + 1])
                ins.then_inc(s.var, 1)
                act.wait_ge(s.var, ch + 1)
                nc.scalar.activation(st[:, b, 3, :], st[:, b, 2, :], ACT.Sqrt, bias=eps_col[:, 0:1], scale=1.0 / FEAT
                                     ).then_inc(s.root, 1)

            def tail(ch, it, b):
                def rows(i):
                    n, k = ch * CH + i, (b * CH + i) % 2
                    act.wait_ge(s.tab_mm, n + 1)
                    nc.scalar.activation(tab[:, b, i, :], ps[:, 6 + k, 0:FEAT], ACT.Copy,
                                         scale=z_all[:, bass.ds(n, 1)]).then_inc(s.tab, 1)

                wait(act, s.xt_stored[b], 32 * it)
                wait(act, s.stored[b], 16 * it)
                for i in range(CH):
                    n, k = ch * CH + i, (b * CH + i) % 2
                    act.wait_ge(s.xturn, n + 1)
                    c = slice(i * P, (i + 1) * P)
                    nc.scalar.activation(nx_s[:, b, c], ps[0:S0, 4 + k, 0:P], ACT.Copy)
                    nc.scalar.activation(nx_v[:, b, c], ps[0:3 * V0, 4 + k, P:2 * P], ACT.Copy).then_inc(s.xt, 1)
                    if i > 0:
                        rows(i - 1)
                rows(CH - 1)

            def front0(ch, it, b):
                if not (isinstance(it, int) and it == 0 and b == 0):
                    stats(ch - 1, it if b else it - 1, 1 - b)
                if not (isinstance(it, int) and it == 0):
                    tail(ch - 2, it - 1, b)

            if l == 0:
                run_chunks(act, front0)
                stats(NCH - 1, NCH // 2 - 1, 1)
                for b in range(2):
                    tail(NCH - 2 + b, NCH // 2 - 1, b)
            else:
                run_chunks(act, front1, stats)

        TWO_PI = 6.283185307179586
        PI_A = 6.28125
        PI_B = 0.0019350051879882812
        PI_C = TWO_PI - PI_A - PI_B
        ROUND = 12582912.0
        SINE = [(-1) ** (n % 2) / math.factorial(2 * n + 1) for n in range(1, 10)]

        def node_dve(dve, l):
            s = nodes[l]
            if l == 0:
                dve.wait_ge(x_loaded, 16)
            LINKS = 0 if l == 0 else 9 + 1 + 2 * len(SINE[:-2] + [1]) + 2 + 1
            c = [0]

            def front(ch, it, b):
                c[0] = 0

                def S(a, n=1):
                    return st[:, b, a, :] if n == 1 else st[:, b, a:a + n, :]

                if l == 0:
                    for i in range(CH):
                        n, k = ch * CH + i, (b * CH + i) % 2
                        mid_copy(dve, s, n, k, v.tensor_copy)
                        if i == 0:
                            wait(dve, s.root, ch - 1)
                        if i > 0:
                            residual(ch, b, i - 1)
                    residual(ch, b, CH - 1)
                else:
                    z = z_all[:, bass.ds(ch * CH, CH)]
                    ang, turns, red = S(4), S(5, 2), S(7, 2)
                    sq, sine, coef = S(9, 2), S(11, 2), S(13, 2)
                    dve.wait_ge(s.lin_o, (ch + 1) * CH)
                    base = ch * LINKS

                    def link(ins):
                        c[0] += 1
                        ins.then_inc(s.chain, 1)
                        dve.wait_ge(s.chain, base + c[0])

                    link(v.tensor_tensor(ang, lin_o[:, b, :, 2 * FEAT], z, mult))
                    v.tensor_scalar(S(5), ang, 1.0 / TWO_PI, ROUND, mult, add)
                    link(v.tensor_scalar(S(6), ang, 1.0 / TWO_PI, 0.25, mult, add))
                    link(v.tensor_scalar(S(6), S(6), ROUND, None, add))
                    link(v.tensor_scalar(turns, turns, -ROUND, None, add))
                    ang2 = ang.unsqueeze(1).to_broadcast([P, 2, CH])
                    link(v.scalar_tensor_tensor(red, turns, -PI_A, ang2, mult, add))
                    link(v.scalar_tensor_tensor(red, turns, -PI_B, red, mult, add))
                    link(v.scalar_tensor_tensor(red, turns, -PI_C, red, mult, add))
                    link(v.tensor_scalar(S(8), S(8), TWO_PI / 4, None, add))
                    link(v.tensor_tensor(sq, red, red, mult))
                    link(v.tensor_scalar(sine, sq, SINE[-1], SINE[-2], mult, add))
                    for a in SINE[-3::-1] + [1.0]:
                        link(v.tensor_tensor(sine, sine, sq, mult))
                        link(v.tensor_scalar(sine, sine, a, None, add))
                    link(v.tensor_tensor(sine, sine, red, mult))
                    link(v.tensor_tensor(coef, sine, z.unsqueeze(1).to_broadcast([P, 2, CH]), mult))
                    wait(dve, s.root, ch - 1)
                    for i in range(CH):
                        ins = v.scalar_tensor_tensor(pre[:, b, i, :], lin_o[:, b, i, 0:FEAT], st[:, b, 14, i:i + 1],
                                                     x_all[:, bass.ds(ch * CH + i, 1), :].rearrange("p a f -> p (a f)"),
                                                     mult, add)
                    link(ins)
                    for i in range(CH):
                        ins = v.scalar_tensor_tensor(pre[:, b, i, :], lin_o[:, b, i, FEAT:2 * FEAT],
                                                     st[:, b, 13, i:i + 1], pre[:, b, i, :], mult, add,
                                                     accum_out=st[:, b, 0, i:i + 1])
                        ins.then_inc(s.pre, 1)
                dve.wait_ge(s.pre, (ch + 1) * CH)
                v.tensor_scalar(st[:, b, 1, :], st[:, b, 0, :], -1.0 / FEAT, None, mult).then_inc(s.mean, 1)
                assert c[0] == LINKS, (c, LINKS)

            def residual(ch, b, i):
                n, k = ch * CH + i, (b * CH + i) % 2
                dve.wait_ge(s.lin, n + 1)
                v.scalar_tensor_tensor(pre[:, b, i, :], ps[:, 2 + k, 0:FEAT], z_all[:, bass.ds(n, 1)],
                                       x_all[:, bass.ds(n, 1), :].rearrange("p a f -> p (a f)"), mult, add,
                                       accum_out=st[:, b, 0, i:i + 1]).then_inc(s.pre, 1)

            def finish(ch, it, b):
                dve.wait_ge(s.root, ch + 1)
                v.reciprocal(st[:, b, 15, :], st[:, b, 3, :]).then_inc(s.rstd, 1)
                dve.wait_ge(s.rstd, ch + 1)
                if l == 0:
                    wait(dve, s.xturn, (ch - 1) * CH)
                    wait(dve, s.kept, ch - 1)
                else:
                    wait(dve, s.stored[b], 16 * it)
                for i in range(CH):
                    ins = v.tensor_scalar(xn[:, b, i, :], pre[:, b, i, :], st[:, b, 1, i:i + 1], st[:, b, 15, i:i + 1],
                                          add, mult)
                ins.then_inc(s.x, 1)

            run_chunks(dve, front, finish)

        def node_pool(pool, l):
            s = nodes[l]

            def body(it):
                for b in range(2):
                    ch = 2 * it + b
                    pool.wait_ge(s.x, ch + 1)
                    settle(pool)
                    if l == 0:
                        nc.gpsimd.tensor_copy(x_all[:, bass.ds(ch * CH, CH), :], xn[:, b, :, :]).then_inc(s.kept, 1)
                        pool.wait_ge(s.xt, (ch + 1) * CH)
                        cols = bass.ds(ch * CH * P, CH * P)
                        settle(pool)
                        pool.dma_start(x1_t[0:S0, cols], nx_s[:, b, :]).then_inc(s.xt_stored[b], 16)
                        pool.dma_start(x1_t[S0:FEAT, cols], nx_v[:, b, :]).then_inc(s.xt_stored[b], 16)
                        pool.wait_ge(s.tab, (ch + 1) * CH)
                        settle(pool)
                        store_table(pool, 1, b, ch, s.stored[b])
                    else:
                        pool.dma_start(t["out"].rearrange("(n p) f -> p n f", p=P)[:, bass.ds(ch * CH, CH), :],
                                       xn[:, b, :, :]).then_inc(s.stored[b], 16)
            loop(pool, body, NCH // 2)
            for b in range(2):
                pool.wait_ge(s.stored[b], 16 * (NCH // 2))
                if l == 0:
                    pool.wait_ge(s.xt_stored[b], 32 * (NCH // 2))

        def layers_program(eng, edge, general, node):
            phase_barrier(eng)
            outside = eng.value_load(flag_i[0:1, 0:1], min_val=0, max_val=1)
            for l in range(2):
                with eng.If(outside == 0):
                    edge(eng, l)
                with eng.Else():
                    general(eng, l)
                phase_barrier(eng)
                node(eng, l)
                phase_barrier(eng)

        block = ctx.enter_context(nc.Block())

        @block.sync
        def _(sp):
            sp_setup(sp)
            tab_loads(sp)
            layers_program(sp, edge_sp, general_sp, node_sp)

        @block.gpsimd
        def _(pool):
            pool_setup(pool)
            tab_pool(pool)
            layers_program(pool, edge_pool, general_pool, node_pool)

        @block.scalar
        def _(act):
            act_setup(act)
            for l in (1, 0):
                split_first(act, l, "act")
            tab_act(act)
            layers_program(act, edge_act, general_act, node_act)

        @block.vector
        def _(dve):
            dve_constants(dve)
            for l in (1, 0):
                split_first(dve, l, "dve")
            dve_weights(dve)
            dve_windows(dve)
            layers_program(dve, edge_dve, general_dve, node_dve)

        @block.tensor
        def _(pe):
            tab_pe(pe)
            pe_windows(pe)
            layers_program(pe, edge_pe, general_pe, node_pe)


def kernel(**inputs):
    import numpy as np
    import concourse.bacc as bacc
    from concourse.bass_utils import run_bass_kernel_spmd

    a = {k: np.asarray(v) for k, v in inputs.items()}

    def component_major(v):
        return np.concatenate([v[:, :S0], v[:, S0:].reshape(-1, V0, 3).transpose(0, 2, 1).reshape(-1, 3 * V0)], 1)

    def pad_rows(v, n, mode="constant"):
        return np.pad(v, [(0, n - v.shape[0])] + [(0, 0)] * (v.ndim - 1), mode=mode)

    def weights_of_edges(w):
        return np.concatenate([w[:, :S0], w[:, 2 * S0:2 * S0 + V0], w[:, S0:2 * S0], w[:, 2 * S0 + V0:]], 1)

    def three_blocks(w):
        out = np.zeros((3 * V0, 3 * V0), w.dtype)
        for i in range(3):
            out[i * V0:(i + 1) * V0, i * V0:(i + 1) * V0] = w
        return out

    def by_group(v):
        return pad_rows(v, NB * BODY).reshape(2 * NB, GT * P, -1).transpose(0, 2, 1)

    def onto_scalars(w):
        return np.pad(w, [(0, 0), (0, 3 * V0)])

    def onto_vectors(w):
        return np.pad(three_blocks(w), [(0, 0), (S0, 0)])

    def from_messages(w0, w1, w3=None):
        out = np.zeros((4, BLK, FEAT + (w3 is not None)), w0.dtype)
        out[0, :, 0:S0] = w0
        for i in range(3):
            out[i + 1, :, S0 + i * V0:S0 + (i + 1) * V0] = w1
        if w3 is not None:
            out[0, :, FEAT:] = w3
        return out.reshape(MID // P, P, -1).transpose(1, 0, 2)

    x = pad_rows(component_major(a["x"]), NPAD)
    EP = T * P
    src = pad_rows(a["src"], EP)
    dst = pad_rows(a["dst"], EP, "edge")
    tiles = dst.reshape(T, P)
    host = {
        "x_rows": x.reshape(NT, P, FEAT).transpose(1, 0, 2),
        "x_t": x.T,
        "z": pad_rows(a["node_vec1"], NPAD).reshape(NT, P).T,
        "src_pt": src.reshape(T, P).T,
        "dst_pt": tiles.T,
        "dst_first": dst[::GT * P],
        "dst_first_c": dst[::GT * P].reshape(2, HT).T,
        "dst_flat": dst.reshape(1, EP),
        "y": pad_rows(a["edge_attr_4"], EP).reshape(T, P, 4).transpose(1, 0, 2),
        "attr12": by_group(a["edge_attr_12"]),
        "attr8": by_group(a["edge_attr_8"]),
        "L0_fc1": a["L0_gnn_W_fc1"], "L0_fc2": weights_of_edges(a["L0_gnn_W_fc2"]),
        "L0_l1_0": onto_scalars(a["L0_gnn_W_l1_0"]), "L0_l1_1": onto_vectors(a["L0_gnn_W_l1_1"]),
        "L0_sc0": onto_scalars(a["L0_gnn_W_sc0"]), "L0_sc1": onto_vectors(a["L0_gnn_W_sc1"]),
        "L0_l2": from_messages(a["L0_gnn_W_l2_0"], a["L0_gnn_W_l2_1"]),
        "L1_fc1": a["L1_gnn_fc_w1"], "L1_fc2": weights_of_edges(a["L1_gnn_fc_w2"]),
        "L1_l1_0": onto_scalars(a["L1_gnn_lin1_w0"]), "L1_l1_1": onto_vectors(a["L1_gnn_lin1_w1"]),
        "L1_sc0": onto_scalars(a["L1_gnn_sc_w0"]), "L1_sc1": onto_vectors(a["L1_gnn_sc_w1"]),
        "L1_l2": from_messages(a["L1_gnn_lin2_w0"], a["L1_gnn_lin2_w1"], a["L1_gnn_lin3_w"]),
    }
    nc = bacc.Bacc("TRN2", target_bir_lowering=False, num_devices=1)
    arrays, t = {}, {}
    for name, v in host.items():
        arrays[name] = np.ascontiguousarray(v)
        t[name] = nc.dram_tensor(name, arrays[name].shape, mybir.dt.from_np(arrays[name].dtype), kind="ExternalInput").ap()
    t["out"] = nc.dram_tensor("out", [NPAD, FEAT], F32, kind="ExternalOutput").ap()
    program(nc, t)
    r = run_bass_kernel_spmd(nc, [arrays], core_ids=[0])
    out = r.results[0]["out"][:N]
    return np.concatenate([out[:, :S0], out[:, S0:].reshape(N, 3, V0).transpose(0, 2, 1).reshape(N, 3 * V0)], 1)
```
